# Optimizing a Trainium2 kernel written in Bass

```python
import numpy as np
import jax
import jax.numpy as jnp

def _softmax(x, axis=-1):
    return jax.nn.softmax(x, axis=axis)

def _gelu(x):
    return jax.nn.gelu(x, approximate=True)

def _silu(x):
    return jax.nn.silu(x)

def _sigmoid(x):
    return jax.nn.sigmoid(x)

def _layernorm(x, axis=-1, eps=1e-05):
    m = jnp.mean(x, axis=axis, keepdims=True)
    v = jnp.var(x, axis=axis, keepdims=True)
    return (x - m) / jnp.sqrt(v + eps)

def _scatter_add(tgt, idx, src, axis=0):
    return tgt.at[idx].add(src)

def _segment_sum(src, seg, n):
    return jax.ops.segment_sum(src, seg, n)
kernel_name = 'mk_gnn_ffn_d1_gnn_r32_56d0f5'

def setup_inputs(seed: int=0):
    np.random.seed(seed)
    _w = jnp.asarray

    def _rec_inputs():
        import jax
        import jax.numpy as jnp
        _gk = jax.random.key(seed)
        x = -0.0002117 + 1 * jax.random.normal(jax.random.fold_in(_gk, 1), (3125, 256), jnp.float32)
        _s = jax.random.randint(jax.random.fold_in(_gk, 2), (25000,), 0, 3125, jnp.int32)
        _d = jax.random.randint(jax.random.fold_in(_gk, 3), (25000,), 0, 3125, jnp.int32)
        _loop = jnp.arange(3125, dtype=jnp.int32)
        src = jnp.concatenate([_s, _d, _loop])
        dst = jnp.concatenate([_d, _s, _loop])
        _o = jnp.argsort(dst, stable=True)
        src = src[_o]
        dst = dst[_o]
        return (x, src, dst)
    x, src, dst = _rec_inputs()

    def _L0_gnn_setup():
        import jax, jax.numpy as jnp
        import numpy as np
        N_NODES = 3125
        N_EDGES = 50000
        NFEAT, NHID, NCLASS = (256, 512, 256)

        def _init_params(key):
            ks = jax.random.split(key, 8)
            s = 0.02
            p = {'W1a': jax.random.normal(ks[0], (NFEAT, NHID), jnp.float32) * s, 'b1a': jnp.zeros((NHID,), jnp.float32), 'W1b': jax.random.normal(ks[1], (NHID, NHID), jnp.float32) * s, 'b1b': jnp.zeros((NHID,), jnp.float32), 'W2a': jax.random.normal(ks[2], (NHID, NHID), jnp.float32) * s, 'b2a': jnp.zeros((NHID,), jnp.float32), 'W2b': jax.random.normal(ks[3], (NHID, NCLASS), jnp.float32) * s, 'b2b': jnp.zeros((NCLASS,), jnp.float32), 'eps1': jnp.zeros((), jnp.float32), 'eps2': jnp.zeros((), jnp.float32)}
            return p

        def _gin_agg(h, src, dst, eps, n_nodes):
            agg = jax.ops.segment_sum(h[src], dst, num_segments=n_nodes)
            return (1.0 + eps) * h + agg
        key = jax.random.key(seed)
        kx, ke, kp = jax.random.split(key, 3)
        x = jax.random.normal(kx, (N_NODES, NFEAT), jnp.float32)
        edge_index = jax.random.randint(ke, (2, N_EDGES), 0, N_NODES, jnp.int64)
        inp = {'x': x, 'edge_index': edge_index}
        inp.update(_init_params(kp))
        return inp
    _L0_gnn_all = _L0_gnn_setup()
    _L0_gnn_in = {k: v for k, v in _L0_gnn_all.items() if k in ('W1a', 'b1a', 'W1b', 'b1b', 'W2a', 'b2a', 'W2b', 'b2b', 'eps1', 'eps2')}
    del _L0_gnn_all

    def _L0_ffn_setup():
        import jax, jax.numpy as jnp
        import numpy as np
        B, S, D, E, H, K = (4, 128, 256, 8, 512, 2)
        key = jax.random.key(seed)
        ks = jax.random.split(key, 6)
        x = jax.random.normal(ks[0], (B, S, D), jnp.float32)
        Wg = jax.random.normal(ks[1], (D, E), jnp.float32) * 0.02
        bg = jnp.zeros((E,), jnp.float32)
        W1 = jax.random.normal(ks[2], (E, D, H), jnp.float32) * 0.02
        b1 = jnp.zeros((E, H), jnp.float32)
        W2 = jax.random.normal(ks[3], (E, H, D), jnp.float32) * 0.02
        b2 = jnp.zeros((E, D), jnp.float32)
        return {'x': x, 'Wg': Wg, 'bg': bg, 'W1': W1, 'b1': b1, 'W2': W2, 'b2': b2}
    _L0_ffn_all = _L0_ffn_setup()
    _L0_ffn_in = {k: v for k, v in _L0_ffn_all.items() if k in ('Wg', 'bg', 'W1', 'b1', 'W2', 'b2')}
    del _L0_ffn_all
    return {'x': x, 'src': src, 'dst': dst, 'L0_gnn_W1a': _L0_gnn_in['W1a'], 'L0_gnn_b1a': _L0_gnn_in['b1a'], 'L0_gnn_W1b': _L0_gnn_in['W1b'], 'L0_gnn_b1b': _L0_gnn_in['b1b'], 'L0_gnn_W2a': _L0_gnn_in['W2a'], 'L0_gnn_b2a': _L0_gnn_in['b2a'], 'L0_gnn_W2b': _L0_gnn_in['W2b'], 'L0_gnn_b2b': _L0_gnn_in['b2b'], 'L0_gnn_eps1': _L0_gnn_in['eps1'], 'L0_gnn_eps2': _L0_gnn_in['eps2'], 'L0_ffn_Wg': _L0_ffn_in['Wg'], 'L0_ffn_bg': _L0_ffn_in['bg'], 'L0_ffn_W1': _L0_ffn_in['W1'], 'L0_ffn_b1': _L0_ffn_in['b1'], 'L0_ffn_W2': _L0_ffn_in['W2'], 'L0_ffn_b2': _L0_ffn_in['b2']}

def reference(x, src, dst, L0_gnn_W1a, L0_gnn_b1a, L0_gnn_W1b, L0_gnn_b1b, L0_gnn_W2a, L0_gnn_b2a, L0_gnn_W2b, L0_gnn_b2b, L0_gnn_eps1, L0_gnn_eps2, L0_ffn_Wg, L0_ffn_bg, L0_ffn_W1, L0_ffn_b1, L0_ffn_W2, L0_ffn_b2):
    import jax
    import jax.numpy as jnp

    def _L0_gnn_ref(x, edge_index, W1a, b1a, W1b, b1b, W2a, b2a, W2b, b2b, eps1, eps2):
        import jax, jax.numpy as jnp
        import numpy as np
        N_NODES = 3125
        N_EDGES = 50000
        NFEAT, NHID, NCLASS = (256, 512, 256)

        def _init_params(key):
            ks = jax.random.split(key, 8)
            s = 0.02
            p = {'W1a': jax.random.normal(ks[0], (NFEAT, NHID), jnp.float32) * s, 'b1a': jnp.zeros((NHID,), jnp.float32), 'W1b': jax.random.normal(ks[1], (NHID, NHID), jnp.float32) * s, 'b1b': jnp.zeros((NHID,), jnp.float32), 'W2a': jax.random.normal(ks[2], (NHID, NHID), jnp.float32) * s, 'b2a': jnp.zeros((NHID,), jnp.float32), 'W2b': jax.random.normal(ks[3], (NHID, NCLASS), jnp.float32) * s, 'b2b': jnp.zeros((NCLASS,), jnp.float32), 'eps1': jnp.zeros((), jnp.float32), 'eps2': jnp.zeros((), jnp.float32)}
            return p

        def _gin_agg(h, src, dst, eps, n_nodes):
            agg = jax.ops.segment_sum(h[src], dst, num_segments=n_nodes)
            return (1.0 + eps) * h + agg
        src, dst = (edge_index[0], edge_index[1])
        n = x.shape[0]
        h = _gin_agg(x, src, dst, eps1, n)
        h = jax.nn.relu(h @ W1a + b1a)
        h = jax.nn.relu(h @ W1b + b1b)
        h = _gin_agg(h, src, dst, eps2, n)
        h = jax.nn.relu(h @ W2a + b2a)
        out = h @ W2b + b2b
        return out

    def _L0_ffn_ref(x, Wg, bg, W1, b1, W2, b2):
        import jax, jax.numpy as jnp
        import numpy as np
        B, S, D, E, H, K = (4, 128, 256, 8, 512, 2)
        Bv, Sv, Dv = x.shape
        gate_scores = x @ Wg + bg
        _, idx = jax.lax.top_k(gate_scores, K)
        mask = jax.nn.one_hot(idx, E, dtype=x.dtype).sum(axis=-2)
        xf = x.reshape(-1, Dv)
        mf = mask.reshape(-1, E)
        h = jax.nn.gelu(jnp.einsum('td,edh->teh', xf, W1) + b1[None], approximate=False)
        y = jnp.einsum('teh,ehd->ted', h, W2) + b2[None]
        out = jnp.einsum('ted,te->td', y, mf)
        return out.reshape(Bv, Sv, Dv)
    edge_index = jnp.stack([src, dst])
    x = x + _L0_gnn_ref(_layernorm(x, axis=-1), edge_index, L0_gnn_W1a, L0_gnn_b1a, L0_gnn_W1b, L0_gnn_b1b, L0_gnn_W2a, L0_gnn_b2a, L0_gnn_W2b, L0_gnn_b2b, L0_gnn_eps1, L0_gnn_eps2)
    x = x + _L0_ffn_ref(_layernorm(x, axis=-1)[None], L0_ffn_Wg, L0_ffn_bg, L0_ffn_W1, L0_ffn_b1, L0_ffn_W2, L0_ffn_b2)[0]
    return x

_drawn_inputs = setup_inputs


def setup_inputs(seed=0):
    import zlib

    import numpy as np

    out = dict(_drawn_inputs(seed))
    spreads = {'L0_gnn_b1a': (0.0, 0.1),
     'L0_gnn_b1b': (0.0, 0.1),
     'L0_gnn_b2a': (0.0, 0.1),
     'L0_gnn_b2b': (0.0, 0.1),
     'L0_ffn_bg': (0.0, 0.1),
     'L0_ffn_b1': (0.0, 0.282),
     'L0_ffn_b2': (0.0, 0.1)}
    factors = {}
    for name, (base, spread) in spreads.items():
        noise = np.random.default_rng([zlib.crc32(name.encode()), seed]).standard_normal(out[name].shape)
        drawn = base * np.exp(spread * noise) if base else spread * noise
        out[name] = jnp.asarray(drawn.astype(out[name].dtype))
    for name, factor in factors.items():
        out[name] = (out[name] * factor).astype(out[name].dtype)
    return out
```

```python
from contextlib import ExitStack

import concourse.bass as bass
from concourse import mybir

F32 = mybir.dt.float32
I32 = mybir.dt.int32
ALU = mybir.AluOpType
ACT = mybir.ActivationFunctionType
AX_X = mybir.AxisListType.X
ds = bass.ds

P = 128
LN_EPS = 1e-5
U = 9
AGB = 3
GT = 5


def gnn_moe_kernel(nc, x, src, dst, W1a, b1a, W1b, b1b, W2a, b2a, W2b, b2b, eps1, eps2,
                   Wg, bg, W1, b1, W2, b2, out):
    N, D = x.shape
    H = W1a.shape[1]
    E = Wg.shape[1]
    EDGES = src.shape[0]
    TILES = -(-N // P)
    FULL = N // P
    TAIL = N - FULL * P
    NP = TILES * P
    CHUNKS = -(-EDGES // P)
    EFULL = EDGES // P
    ETAIL = EDGES - EFULL * P
    ITEMS = CHUNKS + TILES
    TURNS = ITEMS // U
    GROUPS = TILES // GT
    GN = GT * P
    HALF = GN // 2
    KD, KH = D // P, H // P
    BLK = 4
    EP = next(p for p in range(P, 0, -1) if EDGES % p == 0)
    EC = EDGES // EP
    assert ITEMS == TURNS * U and TILES == GROUPS * GT and ITEMS + U <= BLK * P and U % AGB == 0
    assert H == 512 and D == 256 and E == 8 and ETAIL > 0 and TAIL > 0 and EFULL == CHUNKS - 1

    with ExitStack() as ctx:
        def sb(name, shape, dt=F32):
            return ctx.enter_context(nc.sbuf_tensor(name, shape, dt))

        def sem(name):
            return ctx.enter_context(nc.semaphore(name))

        xn_d = nc.dram_tensor("xn_d", [NP, D], F32).ap()
        h_d = nc.dram_tensor("h_d", [NP, H], F32).ap()
        edges_d = nc.dram_tensor("edges_d", [CHUNKS + 1, 2 * P], I32).ap()
        item_tile_d = nc.dram_tensor("item_tile_d", [BLK * P], I32).ap()

        xs = sb("xs", [P, TILES, D])
        acc1 = sb("acc1", [P, TILES, D])
        acc2 = sb("acc2", [P, TILES, H])
        ring = sb("ring", [P, U, H])
        xnT = acc1[:, :, :].rearrange("p t d -> p (t d)").rearrange("p (k n) -> p k n", k=KD)
        tmp = acc2[:, :, :].rearrange("p t d -> p (t d)")
        dst_i = tmp[0:EP, 0:EC].bitcast(I32)
        dst_f = tmp[0:EP, EC:2 * EC]
        below = [tmp[0:EP, (t + 1) * EC:(t + 2) * EC] for t in range(TILES)]
        early = ring[:, :, :].rearrange("p u d -> p (u d)")
        item_edges_i = early[:, 0:BLK * 2 * P].bitcast(I32).rearrange("p (b c) -> p b c", b=BLK)
        item_edges_f = early[:, BLK * 2 * P:2 * BLK * 2 * P].rearrange("p (b c) -> p b c", b=BLK)
        w1a = sb("w1a", [P, KD, H])
        w1b = sb("w1b", [P, KH, H])
        w2a = sb("w2a", [P, KH, H])
        w2b = sb("w2b", [P, KH, D])
        wg = sb("wg", [P, KD, E])
        b1a_c = sb("b1a_c", [P, KH])
        b2a_c = sb("b2a_c", [P, KH])
        b1_c = sb("b1_c", [P, E, KH])
        b1b_r = sb("b1b_r", [1, H])
        b2b_r = sb("b2b_r", [1, D])
        bg_r = sb("bg_r", [1, E])
        b2_e = sb("b2_e", [E, D])
        scale1 = sb("scale1", [P, 1])
        scale2 = sb("scale2", [P, 1])
        we1 = sb("we1", [P, 2, KD, H])
        we2 = sb("we2", [P, 2, KH, D])
        ident = sb("ident", [P, P])
        ones = sb("ones", [P, P])
        node_id = sb("node_id", [P, P])
        item_id = sb("item_id", [P, BLK])
        expert_id = sb("expert_id", [P, E])
        pad_rows = sb("pad_rows", [2, 2 * P], I32)
        cnt = sb("cnt", [P, TILES])
        bound = sb("bound", [P, TILES + 1])
        bound_i = sb("bound_i", [P, 2, TILES + 1], I32)
        chunk_lo = sb("chunk_lo", [P, 2, TILES])
        per_tile = sb("per_tile", [P, 6, TILES])
        item_cmp = sb("item_cmp", [P, 2, BLK, TILES - 1])
        item_sum = sb("item_sum", [P, 6, BLK])
        item_chunk_i = sb("item_chunk_i", [P, BLK], I32)
        item_tile_i = sb("item_tile_i", [P, BLK], I32)
        item_tile_r = sb("item_tile_r", [1, BLK * P], I32)
        src_col = sb("src_col", [P, BLK * P], I32)
        dst_col = sb("dst_col", [P, BLK * P])
        idx = sb("idx", [P, U], I32)
        onehot = sb("onehot", [P, U, P])
        stats = sb("stats", [P, TILES, 6])
        mv = sb("mv", [P, TILES, 2])
        ln = sb("ln", [P, 5, TILES])
        stage = sb("stage", [P, 2, H])
        aT = sb("aT", [P, KH, GN])
        hT = sb("hT", [P, KH, GN])
        hb = ring[:, 0:GT, :]
        x2 = ring[:, :, :].rearrange("p u d -> p (u d)")[:, 0:GT * D].rearrange("p (t d) -> p t d", t=GT)
        xn2 = ring[:, :, :].rearrange("p u d -> p (u d)")[:, GT * D:2 * GT * D].rearrange("p (t d) -> p t d", t=GT)
        gates = sb("gates", [P, GT, E])
        top = sb("top", [P, GT, E])
        top_i = sb("top_i", [P, GT, E], mybir.dt.uint32)
        top_f = sb("top_f", [P, GT, E])
        pick = sb("pick", [P, GT, E])
        mask_g = sb("mask_g", [P, GT, E])
        maskT = sb("maskT", [E, GT, P])
        mask = sb("mask", [P, TILES, E])

        bank = [ctx.enter_context(nc.psum_tensor(f"bank{i}", [P, 512], F32)) for i in range(8)]

        s = {}

        def S(name):
            if name not in s:
                s[name] = sem(name)
            return s[name]

        x_in, edges_in, pad_made, pad_put, dst_in = S("x_in"), S("edges_in"), S("pad_made"), S("pad_put"), S("dst_in")
        consts, weights_in, prep, cnt_sum = S("consts"), S("weights_in"), S("prep"), S("cnt_sum")
        chunk_ids, items_in, items_T, tiles_out, tiles_in = (
            S("chunk_ids"), S("items_in"), S("items_T"), S("tiles_out"), S("tiles_in"))
        cols_made, tile_made = S("cols_made"), S("tile_made")
        stats_made, var_made, root_made, rstd_made, xn_made, xn_put, acc1_scaled = (
            S("stats_made"), S("var_made"), S("root_made"), S("rstd_made"), S("xn_made"), S("xn_put"), S("acc1_scaled"))
        gathered = [[S(f"gathered{L}_{u}") for u in range(U)] for L in range(2)]
        idx_ready = [S(f"idx_ready{L}") for L in range(2)]
        onehot_ready = [S(f"onehot_ready{L}") for L in range(2)]
        item_summed = [S(f"item_summed{L}") for L in range(2)]
        item_added = [S(f"item_added{L}") for L in range(2)]
        staged = [S(f"staged{L}") for L in range(2)]
        turned = [S(f"turned{L}") for L in range(2)]
        turned_out = [S(f"turned_out{L}") for L in range(2)]
        up = [S(f"up{L}") for L in range(3)]
        up_out = [S(f"up_out{L}") for L in range(3)]
        down = [S(f"down{L}") for L in range(3)]
        down_out = [S(f"down_out{L}") for L in range(2)]
        h_made, h_scaled = S("h_made"), S("h_scaled")
        h_put = [S(f"h_put{j}") for j in range(GT)]
        x2_stats, x2_var, x2_root, x2_rstd, xn2_made = S("x2_stats"), S("x2_var"), S("x2_root"), S("x2_rstd"), S("xn2_made")
        xn2_turned, xn2_out, gate_sum, gate_out = S("xn2_turned"), S("xn2_out"), S("gate_sum"), S("gate_out")
        topped, masked, mask_turned, mask_T, bias2, moe_added, x2_kept = (
            S("topped"), S("masked"), S("mask_turned"), S("mask_T"), S("bias2"), S("moe_added"), S("x2_kept"))
        xnT_kept = S("xnT_kept")
        expert_in = [S(f"expert_in{i}") for i in range(2)]
        out_put = S("out_put")
        dve = S("dve")

        block = ctx.enter_context(nc.Block())

        @block.sync
        def _(sp):
            tail_rows = x[FULL * P:N, :]
            sp.dma_start(dst_i, dst.rearrange("(p c) -> p c", p=EP)).then_inc(dst_in, 16)
            sp.wait_ge(pad_made, 3)
            sp.dma_start(edges_d[CHUNKS - 1:CHUNKS + 1, :], pad_rows[:, :]).then_inc(pad_put, 16)
            sp.dma_start(xs[:, 0:FULL, :], x[0:FULL * P, :].rearrange("(t p) d -> p t d", p=P)).then_inc(x_in, 16)
            sp.dma_start(xs[0:TAIL, FULL, :], tail_rows).then_inc(x_in, 16)
            for c, a in enumerate((src, dst)):
                sp.dma_start(edges_d[0:EFULL, c * P:c * P + P],
                             a[0:EFULL * P].rearrange("(c e) -> c e", e=P)).then_inc(edges_in, 16)
            sp.wait_ge(pad_put, 16)
            for c, a in enumerate((src, dst)):
                sp.dma_start(edges_d[EFULL:EFULL + 1, c * P:c * P + ETAIL],
                             a[EFULL * P:EDGES].rearrange("(c e) -> c e", c=1)).then_inc(edges_in, 16)
            with nc.allow_non_contiguous_dma(reason="biases as columns, one scalar for all partitions"):
                loads = [
                    (scale1[:, :], eps1.rearrange("(a b) -> a b", a=1).to_broadcast([P, 1])),
                    (scale2[:, :], eps2.rearrange("(a b) -> a b", a=1).to_broadcast([P, 1])),
                    (w1a[:, :, :], W1a.rearrange("(k p) n -> p k n", p=P)),
                    (w1b[:, :, :], W1b.rearrange("(k p) n -> p k n", p=P)),
                    (w2a[:, :, :], W2a.rearrange("(k p) n -> p k n", p=P)),
                    (w2b[:, :, :], W2b.rearrange("(k p) n -> p k n", p=P)),
                    (wg[:, :, :], Wg.rearrange("(k p) n -> p k n", p=P)),
                    (b1a_c[:, :], b1a.rearrange("(k p) -> p k", p=P)),
                    (b2a_c[:, :], b2a.rearrange("(k p) -> p k", p=P)),
                    (b1_c[:, :, :], b1.rearrange("e (k p) -> p e k", p=P)),
                    (b1b_r[:, :], b1b.rearrange("(a n) -> a n", a=1)),
                    (b2b_r[:, :], b2b.rearrange("(a n) -> a n", a=1)),
                    (bg_r[:, :], bg.rearrange("(a n) -> a n", a=1)),
                    (b2_e[:, :], b2),
                ]
                for to, of in loads:
                    sp.dma_start(to, of).then_inc(weights_in, 16)
                sp.wait_ge(tile_made, 1)
                sp.dma_start(item_tile_d.rearrange("(b p) -> p b", p=P), item_tile_i[:, :]).then_inc(tiles_out, 16)
            sp.wait_ge(tiles_out, 16)
            sp.dma_start(item_tile_r[:, :], item_tile_d.rearrange("(a n) -> a n", a=1)).then_inc(tiles_in, 16)
            sp.wait_ge(xn_made, TILES)
            sp.dma_start(xn_d.rearrange("(t p) d -> p t d", p=P), acc1[:, :, :]).then_inc(xn_put, 16)
            with sp.Fori(0, GROUPS) as g:
                for j in range(GT):
                    sp.wait_ge(h_made, g * GT + (j + 1))
                    sp.dma_start(h_d.rearrange("(t p) d -> t p d", p=P)[ds(g * GT + j, 1), :, :].rearrange("t p d -> (t p) d"),
                                 hb[:, j, :]).then_inc(h_put[j], 16)

            def load_expert(e, b):
                sp.dma_start(we1[:, b, :, :], W1[ds(e, 1), :, :].rearrange("e (k p) n -> p (e k) n", p=P)).then_inc(expert_in[b], 16)
                sp.dma_start(we2[:, b, :, :], W2[ds(e, 1), :, :].rearrange("e (k p) n -> p (e k) n", p=P)).then_inc(expert_in[b], 16)
            load_expert(0, 0)
            load_expert(1, 1)
            with sp.Fori(1, E // 2) as q:
                for b in range(2):
                    sp.wait_ge(down[2], q * (2 * TILES) + (b - 1) * TILES)
                    load_expert(q * 2 + b, b)
            sp.wait_ge(moe_added, (E + 1) * TILES)
            sp.dma_start(out[0:FULL * P, :].rearrange("(t p) d -> p t d", p=P), xs[:, 0:FULL, :]).then_inc(out_put, 16)
            sp.dma_start(out[FULL * P:N, :], xs[0:TAIL, FULL, :]).then_inc(out_put, 16)
            sp.wait_ge(out_put, 32)
            sp.wait_ge(weights_in, 16 * 14)

        @block.gpsimd
        def _(pool):
            pool.memset(pad_rows[:, 0:P], 0).then_inc(pad_made, 1)
            pool.memset(pad_rows[:, P:2 * P], -1).then_inc(pad_made, 1)
            pool.memset(xs[:, FULL, :], 0.0).then_inc(pad_made, 1)
            pool.memset(ident[:, :], 0.0).then_inc(consts, 1)
            pool.memset(ones[:, :], 1.0).then_inc(consts, 1)
            for t, n in ((node_id, P), (expert_id, E)):
                pool.iota(t[:, :], [[1, n]], base=0, channel_multiplier=0,
                          allow_small_or_imprecise_dtypes=True).then_inc(consts, 1)
            pool.iota(item_id[:, :], [[P, BLK]], base=0, channel_multiplier=1,
                      allow_small_or_imprecise_dtypes=True).then_inc(consts, 1)
            pool.wait_ge(consts, 5)
            pool.affine_select(out=ident[:, :], in_=ident[:, :], compare_op=ALU.not_equal, fill=1.0,
                               base=0, pattern=[[-1, P]], channel_multiplier=1).then_inc(consts, 1)
            pool.wait_ge(edges_in, 64)
            pool.wait_ge(pad_put, 16)
            pool.wait_ge(chunk_ids, 1)
            for b in range(BLK):
                pool.indirect_dma_start(item_edges_i[:, b, :], None, edges_d[:, :],
                                        bass.IndirectOffsetOnAxis(item_chunk_i[:, b:b + 1], 0)).then_inc(items_in, 16)

            def gathers(L, i0):
                table, W = ((xn_d, D), (h_d, H))[L]
                for u in range(U):
                    pool.wait_ge(idx_ready[L], i0 + (u + 1))
                    pool.nop(nofuse=True)
                    pool.indirect_dma_start(ring[:, u, 0:W], None, table[:, :],
                                            bass.IndirectOffsetOnAxis(idx[:, u:u + 1], 0)).then_inc(gathered[L][u], 16)

            def stage_tiles(L):
                acc, W = ((acc1, D), (acc2, H))[L]
                if L == 0:
                    pool.wait_ge(item_added[0], ITEMS)
                else:
                    pool.wait_ge(item_added[1], ITEMS)
                for j in range(2):
                    pool.tensor_copy(stage[:, j, 0:W], acc[:, j, :]).then_inc(staged[L], 1)
                with pool.Fori(2, TILES - 1, 2) as t:
                    for j in range(2):
                        pool.wait_ge(turned[L], t + (j - 1))
                        pool.tensor_copy(stage[:, j, 0:W], acc[:, ds(t + j, 1), :].rearrange("p t d -> p (t d)")).then_inc(staged[L], 1)
                pool.wait_ge(turned[L], TILES - 2)
                pool.tensor_copy(stage[:, 0, 0:W], acc[:, TILES - 1, :]).then_inc(staged[L], 1)

            pool.wait_ge(xn_put, 16)
            with pool.Fori(0, TURNS) as n:
                gathers(0, n * U)
            stage_tiles(0)
            for j in range(GT):
                pool.wait_ge(h_put[j], 16 * GROUPS)
            pool.wait_ge(down_out[0], TILES)
            with pool.Fori(0, TURNS) as n:
                gathers(1, n * U)
            stage_tiles(1)

        @block.scalar
        def _(act):
            act.wait_ge(var_made, 1)
            act.activation(ln[:, 1, :], ln[:, 0, :], ACT.Sqrt).then_inc(root_made, 1)

            def ids(L, i0, first):
                for u in range(U):
                    if not first:
                        act.wait_ge(item_summed[L], i0 + (u + 1 - U))
                    i = i0 + u
                    act.copy(idx[:, u:u + 1], src_col[:, ds(i, 1)]).then_inc(idx_ready[L], 1)

            def all_ids(L):
                ids(L, 0, True)
                with act.Fori(1, TURNS) as n:
                    ids(L, n * U, False)

            def mlp(L, g):
                K = (KD, KH)[L]
                bias = (b1a_c, b2a_c)[L]
                for j in range(GT):
                    act.wait_ge(turned[L], g * GT + (j + 1))
                    act.copy(aT[:, 0:K, j * P:j * P + P],
                             bank[j % 2][:, 0:K * P].rearrange("p (k n) -> p k n", k=K)).then_inc(turned_out[L], 1)
                for u in range(2 * KH):
                    m, half = u // 2, u % 2
                    act.wait_ge(up[L], g * (2 * KH) + (u + 1))
                    act.activation(hT[:, m, half * HALF:half * HALF + HALF], bank[2 + u % 4][:, 0:HALF], ACT.Relu,
                                   bias=bias[:, m:m + 1]).then_inc(up_out[L], 1)

            act.wait_ge(cols_made, 2)
            all_ids(0)
            act.wait_ge(weights_in, 16 * 14)

            def hidden(g, first):
                mlp(0, g)
                for j in range(GT):
                    act.wait_ge(down[0], g * GT + (j + 1))
                    if not first:
                        act.wait_ge(h_put[j], g * 16)
                        act.wait_ge(down_out[0], g * GT)
                    act.activation(hb[:, j, :], bank[6 + j % 2][:, :], ACT.Relu).then_inc(h_made, 1)

            hidden(0, True)
            with act.Fori(1, GROUPS) as g:
                hidden(g, False)
            all_ids(1)
            with act.Fori(0, GROUPS) as g:
                mlp(1, g)
                act.wait_ge(x2_var, g + 1)
                act.activation(ln[:, 1, 0:GT], ln[:, 0, 0:GT], ACT.Sqrt).then_inc(x2_root, 1)
                for j in range(GT):
                    act.wait_ge(xn2_turned, g * GT + (j + 1))
                    act.copy(aT[:, 0:KD, j * P:j * P + P],
                             bank[j % 2][:, 0:KD * P].rearrange("p (k n) -> p k n", k=KD)).then_inc(xn2_out, 1)
                act.wait_ge(xn2_out, g * GT + GT)
                act.copy(xnT[:, :, ds(g * GN, GN)], aT[:, 0:KD, :]).then_inc(xnT_kept, 1)
                for j in range(GT):
                    act.wait_ge(mask_turned, g * GT + (j + 1))
                    act.copy(maskT[:, j, :], bank[j % 2][0:E, 0:P]).then_inc(mask_T, 1)
            with act.Fori(0, E // 2) as q:
                for b in range(2):
                    with act.Fori(0, GROUPS) as g:
                        for u in range(2 * KH):
                            m, half = u // 2, u % 2
                            act.wait_ge(up[2], q * (4 * GROUPS * KH) + g * (2 * KH) + (b * 2 * GROUPS * KH + u + 1))
                            act.nop(nofuse=True)
                            act.activation(hT[:, m, half * HALF:half * HALF + HALF], bank[2 + u % 4][:, 0:HALF], ACT.Gelu,
                                           bias=b1_c[:, ds(q * 2 + b, 1), m:m + 1].rearrange("p e k -> p (e k)")).then_inc(up_out[2], 1)

        @block.tensor
        def _(pe):
            pe.wait_ge(consts, 6)
            pe.wait_ge(prep, 1)
            pe.matmul(bank[0][:, 0:TILES - 1], ones[0:EP, :], cnt[0:EP, 0:TILES - 1], start=True, stop=True).then_inc(cnt_sum, 1)
            pe.wait_ge(prep, 2)
            for b in range(BLK):
                for c in range(2):
                    pe.transpose(bank[1 + c][:, b * P:b * P + P], item_edges_f[:, b, c * P:c * P + P],
                                 ident[:, :]).then_inc(items_T, 1)

            def sums(L, n, first):
                W = (D, H)[L]
                for u in range(U):
                    i1 = n * U + (u + 1)
                    pe.wait_ge(gathered[L][u], n * 16 + 16)
                    pe.wait_ge(onehot_ready[L], i1)
                    if not (first and u < AGB):
                        pe.wait_ge(item_added[L], i1 - AGB)
                    pe.matmul(bank[3 + u % AGB][:, 0:W], onehot[:, u, :], ring[:, u, 0:W],
                              start=True, stop=True).then_inc(item_summed[L], 1)

            def all_sums(L):
                sums(L, 0, True)
                with pe.Fori(1, TURNS) as n:
                    sums(L, n, False)

            def mlp(L, g):
                K = (KD, KH)[L]
                w = (w1a, w2a)[L]
                wd = (w1b, w2b)[L]
                row = (b1b_r, b2b_r)[L]
                W = (H, D)[L]
                for j in range(GT):
                    pe.wait_ge(staged[L], g * GT + (j + 1))
                    if j >= 2:
                        pe.wait_ge(turned_out[L], g * GT + (j - 1))
                    for k in range(K):
                        mm = pe.transpose(bank[j % 2][:, k * P:k * P + P], stages[L](g, j)[:, k * P:k * P + P], ident[:, :])
                    mm.then_inc(turned[L], 1)
                pe.wait_ge(turned_out[L], g * GT + GT)
                for u in range(2 * KH):
                    m, half = u // 2, u % 2
                    if u >= 4:
                        pe.wait_ge(up_out[L], g * (2 * KH) + (u - 3))
                    for k in range(K):
                        mm = pe.matmul(bank[2 + u % 4][:, 0:HALF], w[:, k, m * P:m * P + P],
                                       aT[:, k, half * HALF:half * HALF + HALF], start=(k == 0), stop=(k == K - 1))
                    mm.then_inc(up[L], 1)
                pe.wait_ge(up_out[L], g * (2 * KH) + 2 * KH)
                for j in range(GT):
                    if j >= 2:
                        pe.wait_ge(down_out[L], g * GT + (j - 1))
                        if L == 0:
                            pe.wait_ge(h_made, g * GT + (j - 1))
                    for k in range(KH):
                        pe.matmul(bank[6 + j % 2][:, 0:W], hT[:, k, j * P:j * P + P], wd[:, k, :],
                                  start=(k == 0), stop=False)
                    pe.matmul(bank[6 + j % 2][:, 0:W], ones[0:1, :], row[:, :], start=False, stop=True).then_inc(down[L], 1)
                pe.wait_ge(down_out[L], g * GT + GT)
                if L == 0:
                    pe.wait_ge(h_made, g * GT + GT)

            stages = [lambda g, j: stage[:, 0, :], lambda g, j: stage[:, 0, :]]
            all_sums(0)
            pe.wait_ge(weights_in, 16 * 14)
            def grp(L, g, par):
                stages[L] = lambda g, j: stage[:, (j + par) % 2, :]
                mlp(L, g)
                if L == 1:
                    gate(g)

            def gate(g):
                pe.wait_ge(xn2_made, g + 1)
                for j in range(GT):
                    if j >= 2:
                        pe.wait_ge(xn2_out, g * GT + (j - 1))
                    for k in range(KD):
                        mm = pe.transpose(bank[j % 2][:, k * P:k * P + P], xn2[:, j, k * P:k * P + P], ident[:, :])
                    mm.then_inc(xn2_turned, 1)
                pe.wait_ge(xn2_out, g * GT + GT)
                for j in range(GT):
                    for k in range(KD):
                        pe.matmul(bank[2][:, j * E:j * E + E], aT[:, k, j * P:j * P + P], wg[:, k, :],
                                  start=(k == 0), stop=False)
                    mm = pe.matmul(bank[2][:, j * E:j * E + E], ones[0:1, :], bg_r[:, :], start=False, stop=True)
                mm.then_inc(gate_sum, 1)
                pe.wait_ge(masked, g + 1)
                for j in range(GT):
                    if j >= 2:
                        pe.wait_ge(mask_T, g * GT + (j - 1))
                    pe.transpose(bank[j % 2][0:E, 0:P], mask_g[:, j, :], ident[:, :]).then_inc(mask_turned, 1)
                for j in range(GT):
                    pe.wait_ge(mask_T, g * GT + (j + 1))
                    if j >= 2:
                        pe.wait_ge(moe_added, g * GT + (j - 1))
                    pe.matmul(bank[6 + j % 2][:, 0:D], maskT[:, j, :], b2_e[:, :], start=True, stop=True).then_inc(bias2, 1)
                pe.wait_ge(moe_added, g * GT + GT)
                pe.wait_ge(xnT_kept, g + 1)

            for L in range(2):
                if L == 1:
                    all_sums(1)
                with pe.Fori(0, GROUPS - 1, 2) as g:
                    grp(L, g, 0)
                    grp(L, g + 1, 1)
                grp(L, GROUPS - 1, 0)
            with pe.Fori(0, E // 2) as q:
                for b in range(2):
                    pe.wait_ge(expert_in[b], q * 32 + 32)
                    pe.nop(nofuse=True)
                    with pe.Fori(0, GROUPS) as g:
                        base = q * (4 * GROUPS * KH) + g * (2 * KH) + b * 2 * GROUPS * KH
                        for u in range(2 * KH):
                            m, half = u // 2, u % 2
                            if u >= 4:
                                pe.wait_ge(up_out[2], base + (u - 3))
                            for k in range(KD):
                                mm = pe.matmul(bank[2 + u % 4][:, 0:HALF], we1[:, b, k, m * P:m * P + P],
                                               xnT[:, k, ds(g * GN + half * HALF, HALF)], start=(k == 0), stop=(k == KD - 1))
                            mm.then_inc(up[2], 1)
                        pe.wait_ge(up_out[2], base + 2 * KH)
                        base = q * (2 * TILES) + g * GT + b * TILES
                        for j in range(GT):
                            if j >= 2:
                                pe.wait_ge(moe_added, base + (TILES + j - 1))
                            for k in range(KH):
                                mm = pe.matmul(bank[6 + j % 2][:, 0:D], hT[:, k, j * P:j * P + P], we2[:, b, k, :],
                                               start=(k == 0), stop=(k == KH - 1))
                            mm.then_inc(down[2], 1)
                        pe.wait_ge(moe_added, base + (TILES + GT))

        @block.vector
        def _(v):
            made = [0]

            def then(ins):
                made[0] += 1
                ins.then_inc(dve, 1)
                v.wait_ge(dve, made[0])

            v.wait_ge(dst_in, 16)
            then(v.tensor_copy(dst_f, dst_i))
            for t in range(1, TILES):
                ins = v.tensor_scalar(below[t], dst_f, float(t * P), None, ALU.is_lt, ALU.add, accum_out=cnt[0:EP, t - 1:t])
            ins.then_inc(prep, 1)
            v.memset(bound[:, 0:1], 0.0)
            v.memset(bound[:, TILES:TILES + 1], float(EDGES))
            v.wait_ge(cnt_sum, 1)
            then(v.tensor_copy(bound[:, 1:TILES], bank[0][:, 0:TILES - 1]))
            v.tensor_copy(bound_i[:, 0, :], bound[:, :])
            then(v.tensor_scalar(bound_i[:, 1, :], bound[:, :], float(P - 1), None, ALU.add))
            then(v.tensor_scalar(bound_i[:, :, :], bound_i[:, :, :], 7, None, ALU.arith_shift_right))
            v.tensor_copy(chunk_lo[:, 0, :], bound_i[:, 0, 0:TILES])
            then(v.tensor_copy(chunk_lo[:, 1, :], bound_i[:, 1, 1:TILES + 1]))
            n_, end_, start_, off_, step_ = (per_tile[:, k, :] for k in range(5))
            then(v.tensor_tensor(n_, chunk_lo[:, 1, :], chunk_lo[:, 0, :], ALU.subtract))
            then(v.tensor_tensor_scan(end_, n_, n_, 0.0, ALU.add, ALU.bypass))
            then(v.tensor_tensor(start_, end_, n_, ALU.subtract))
            then(v.tensor_tensor(off_, chunk_lo[:, 0, :], start_, ALU.subtract))
            then(v.tensor_tensor(step_[:, 1:TILES], off_[:, 1:TILES], off_[:, 0:TILES - 1], ALU.subtract))
            v.wait_ge(consts, 6)
            for b in range(BLK):
                v.tensor_scalar(item_cmp[:, 0, b, :], start_[:, 1:TILES], item_id[:, b:b + 1], None, ALU.is_le)
                ins = v.scalar_tensor_tensor(out=item_cmp[:, 1, b, :], in0=start_[:, 1:TILES], scalar=item_id[:, b:b + 1],
                                             in1=step_[:, 1:TILES], op0=ALU.is_le, op1=ALU.mult)
            then(ins)
            tile_, jump_, past_, chunk_, first_ = (item_sum[:, k, :] for k in range(5))
            v.tensor_reduce(tile_, item_cmp[:, 0, :, :], AX_X, ALU.add)
            v.tensor_reduce(jump_, item_cmp[:, 1, :, :], AX_X, ALU.add)
            then(v.tensor_scalar(past_, item_id[:, :], end_[:, TILES - 1:TILES], float(2 * CHUNKS), ALU.is_ge, ALU.mult))
            v.tensor_copy(item_tile_i[:, :], tile_).then_inc(tile_made, 1)
            then(v.tensor_tensor(chunk_, item_id[:, :], jump_, ALU.add))
            then(v.tensor_tensor(chunk_, chunk_, past_, ALU.add))
            v.tensor_scalar(item_chunk_i[:, :], chunk_, float(CHUNKS), None, ALU.min).then_inc(chunk_ids, 1)
            then(v.tensor_scalar(first_, tile_, float(P), None, ALU.mult))

            v.wait_ge(x_in, 32)
            with v.Fori(0, TILES) as t:
                v.bn_stats(stats[:, ds(t, 1), :].rearrange("p t d -> p (t d)"),
                           xs[:, ds(t, 1), :].rearrange("p t d -> p (t d)")).then_inc(stats_made, 1)
            v.wait_ge(stats_made, TILES)

            def rstd_of(n, roots, roots_value, made_sem, link):
                veps, root, rec, quo, rstd = (ln[:, k, 0:n] for k in range(5))
                mean, half_gap = mv[:, 0:n, 0], mv[:, 0:n, 1]
                st = [stats[:, 0:n, k] for k in range(6)]
                v.tensor_tensor(mean, st[1], st[4], ALU.add)
                v.tensor_tensor(half_gap, st[1], st[4], ALU.subtract)
                link(v.tensor_tensor(veps, st[2], st[5], ALU.add))
                v.tensor_scalar(mean, mean, 0.5, None, ALU.mult)
                link(v.tensor_scalar(half_gap, half_gap, 0.5, None, ALU.mult))
                v.tensor_scalar(veps, veps, 1.0 / D, LN_EPS, ALU.mult, ALU.add)
                link(v.tensor_tensor(half_gap, half_gap, half_gap, ALU.mult))
                v.tensor_tensor(veps, veps, half_gap, ALU.add).then_inc(made_sem, 1)
                v.wait_ge(roots, roots_value)
                link(v.reciprocal(rec, root))
                link(v.tensor_tensor(quo, veps, rec, ALU.mult))
                link(v.tensor_tensor(quo, quo, root, ALU.add))
                link(v.tensor_scalar(quo, quo, 0.5, None, ALU.mult))
                link(v.reciprocal(rstd, quo))

            rstd_of(TILES, root_made, 1, var_made, then)
            with v.Fori(0, TILES) as t:
                v.tensor_scalar(acc1[:, ds(t, 1), :].rearrange("p t d -> p (t d)"),
                                xs[:, ds(t, 1), :].rearrange("p t d -> p (t d)"),
                                mv[:, ds(t, 1), 0:1].rearrange("p t d -> p (t d)"), ln[:, 4, ds(t, 1)],
                                ALU.subtract, ALU.mult).then_inc(xn_made, 1)
            v.wait_ge(items_in, 16 * BLK)
            v.tensor_copy(item_edges_f[:, :, 0:P], item_edges_i[:, :, 0:P])
            for b in range(BLK):
                ins = v.tensor_scalar(item_edges_f[:, b, P:2 * P], item_edges_i[:, b, P:2 * P], first_[:, b:b + 1], None,
                                      ALU.subtract)
            ins.then_inc(prep, 1)
            v.wait_ge(items_T, 2 * BLK)
            v.tensor_copy(src_col[:, :], bank[1][:, :]).then_inc(cols_made, 1)
            v.tensor_copy(dst_col[:, :], bank[2][:, :]).then_inc(cols_made, 1)
            v.wait_ge(weights_in, 16 * 14)
            v.tensor_scalar(scale1[:, :], scale1[:, :], 1.0, None, ALU.add)
            then(v.tensor_scalar(scale2[:, :], scale2[:, :], 1.0, None, ALU.add))
            v.wait_ge(xn_made, TILES)
            v.wait_ge(xn_put, 16)
            then(v.tensor_scalar(acc1[:, :, :], acc1[:, :, :], scale1[:, :], None, ALU.mult))
            v.wait_ge(cols_made, 2)
            v.wait_ge(tiles_in, 16)

            def one_hot(L, i, u):
                v.tensor_scalar(onehot[:, u, :], node_id[:, :], dst_col[:, ds(i, 1)], None,
                                ALU.is_equal).then_inc(onehot_ready[L], 1)

            def add_items(L):
                acc, W = ((acc1, D), (acc2, H))[L]
                for u in range(U):
                    one_hot(L, u, u)
                with v.Fori(0, TURNS) as n:
                    for u in range(U):
                        i = n * U + u
                        t = v.value_load(item_tile_r[0:1, ds(i, 1)], min_val=0, max_val=TILES - 1)
                        at = acc[:, ds(t, 1), :].rearrange("p t d -> p (t d)")
                        v.wait_ge(onehot_ready[L], i + U)
                        v.wait_ge(item_summed[L], i + 1)
                        v.tensor_tensor(at, at, bank[3 + u % AGB][:, 0:W], ALU.add).then_inc(item_added[L], 1)
                        one_hot(L, i + U, u)

            add_items(0)
            with v.Fori(0, GROUPS) as g:
                for j in range(GT):
                    v.wait_ge(h_made, g * GT + (j + 1))
                    v.tensor_scalar(acc2[:, ds(g * GT + j, 1), :].rearrange("p t d -> p (t d)"), hb[:, j, :],
                                    scale2[:, :], None, ALU.mult).then_inc(down_out[0], 1)
            v.wait_ge(down_out[0], TILES)
            add_items(1)
            LINKS = 3 + 5 + 4

            with v.Fori(0, GROUPS) as g:
                for j in range(GT):
                    v.wait_ge(down[1], g * GT + (j + 1))
                    v.tensor_tensor(x2[:, j, :], xs[:, ds(g * GT + j, 1), :].rearrange("p t d -> p (t d)"),
                                    bank[6 + j % 2][:, 0:D], ALU.add).then_inc(down_out[1], 1)
                    v.wait_ge(down_out[1], g * GT + (j + 1))
                    v.bn_stats(stats[:, j, :], x2[:, j, :]).then_inc(x2_stats, 1)
                v.wait_ge(x2_stats, g * GT + GT)
                steps = [0]

                def link(ins):
                    steps[0] += 1
                    ins.then_inc(x2_rstd, 1)
                    v.wait_ge(x2_rstd, g * LINKS + steps[0])

                rstd_of(GT, x2_root, g + 1, x2_var, link)
                for j in range(GT):
                    ins = v.tensor_scalar(xn2[:, j, :], x2[:, j, :], mv[:, j, 0:1], ln[:, 4, j:j + 1],
                                          ALU.subtract, ALU.mult)
                ins.then_inc(xn2_made, 1)
                v.wait_ge(gate_sum, g + 1)
                link(v.tensor_copy(gates[:, :, :], bank[2][:, 0:GT * E].rearrange("p (t e) -> p t e", e=E)))
                v.nop(nofuse=True)
                for j in range(GT):
                    ins = v.max(top[:, j, :], gates[:, j, :])
                link(ins)
                v.nop(nofuse=True)
                for j in range(GT):
                    ins = v.max_index(top_i[:, j, :], top[:, j, :], gates[:, j, :])
                link(ins)
                link(v.tensor_copy(top_f[:, :, :], top_i[:, :, :]))
                assert steps[0] == LINKS
                for j in range(GT):
                    v.tensor_scalar(pick[:, j, :], expert_id[:, :], top_f[:, j, 0:1], None, ALU.is_equal).then_inc(topped, 1)
                    v.wait_ge(topped, g * GT + (j + 1))
                    ins = v.scalar_tensor_tensor(out=mask_g[:, j, :], in0=expert_id[:, :], scalar=top_f[:, j, 1:2],
                                                 in1=pick[:, j, :], op0=ALU.is_equal, op1=ALU.add)
                ins.then_inc(masked, 1)
                v.wait_ge(masked, g + 1)
                v.tensor_copy(mask[:, ds(g * GT, GT), :], mask_g[:, :, :])
                for j in range(GT):
                    v.wait_ge(bias2, g * GT + (j + 1))
                    v.tensor_tensor(xs[:, ds(g * GT + j, 1), :].rearrange("p t d -> p (t d)"), x2[:, j, :],
                                    bank[6 + j % 2][:, 0:D], ALU.add).then_inc(moe_added, 1)
            v.wait_ge(moe_added, TILES)
            with v.Fori(0, E // 2) as q:
                for b in range(2):
                    with v.Fori(0, GROUPS) as g:
                        base = q * (2 * TILES) + g * GT + b * TILES
                        for j in range(GT):
                            v.wait_ge(down[2], base + (j + 1))
                            v.wait_ge(moe_added, base + (TILES + j))
                            at = xs[:, ds(g * GT + j, 1), :].rearrange("p t d -> p (t d)")
                            v.scalar_tensor_tensor(
                                out=at, in0=bank[6 + j % 2][:, 0:D],
                                scalar=mask[:, ds(g * GT + j, 1), ds(q * 2 + b, 1)].rearrange("p t e -> p (t e)"),
                                in1=at, op0=ALU.mult, op1=ALU.add).then_inc(moe_added, 1)


_INS = ['x', 'src', 'dst', 'L0_gnn_W1a', 'L0_gnn_b1a', 'L0_gnn_W1b', 'L0_gnn_b1b', 'L0_gnn_W2a', 'L0_gnn_b2a',
        'L0_gnn_W2b', 'L0_gnn_b2b', 'L0_gnn_eps1', 'L0_gnn_eps2', 'L0_ffn_Wg', 'L0_ffn_bg', 'L0_ffn_W1', 'L0_ffn_b1',
        'L0_ffn_W2', 'L0_ffn_b2']


def kernel(**inputs):
    import numpy as _np
    import concourse.bacc as _bacc
    from concourse import mybir as _mybir
    from concourse.bass_utils import run_bass_kernel_spmd as _run

    nc = _bacc.Bacc("TRN2", target_bir_lowering=False, num_devices=1)
    arrays, args = {}, []
    for name in _INS:
        a = _np.ascontiguousarray(inputs[name]).reshape(_np.shape(inputs[name]) or (1,))
        arrays[f"in_{name}_dram"] = a
        args.append(nc.dram_tensor(f"in_{name}_dram", a.shape, _mybir.dt.from_np(a.dtype), kind="ExternalInput").ap())
    shape = tuple(inputs["x"].shape)
    args.append(nc.dram_tensor("out_0_dram", shape, _mybir.dt.float32, kind="ExternalOutput").ap())
    gnn_moe_kernel(nc, *args)
    r = _run(nc, [arrays], core_ids=[0])
    return r.results[0]["out_0_dram"]
```

```python
from contextlib import ExitStack

import concourse.bass as bass
from concourse import mybir

F32 = mybir.dt.float32
I32 = mybir.dt.int32
ALU = mybir.AluOpType
ACT = mybir.ActivationFunctionType
AX_X = mybir.AxisListType.X
ds = bass.ds

P = 128
LN_EPS = 1e-5
U = 9
AGB = 3
GT = 5
GG = 3
UB = 3


def gnn_moe_kernel(nc, x, src, dst, W1a, b1a, W1b, b1b, W2a, b2a, W2b, b2b, eps1, eps2,
                   Wg, bg, W1, b1, W2, b2, out):
    N, D = x.shape
    H = W1a.shape[1]
    E = Wg.shape[1]
    EDGES = src.shape[0]
    TILES = -(-N // P)
    FULL = N // P
    TAIL = N - FULL * P
    NP = TILES * P
    CHUNKS = -(-EDGES // P)
    EFULL = EDGES // P
    ETAIL = EDGES - EFULL * P
    ITEMS = CHUNKS + TILES
    TURNS = ITEMS // U
    GROUPS = TILES // GT
    GN = GT * P
    KD, KH = D // P, H // P
    BLK = 4
    EP = next(p for p in range(P, 0, -1) if EDGES % p == 0)
    EC = EDGES // EP
    BLOCKS = (2 * NP + E * (P - 1)) // P
    BTURNS = BLOCKS // UB
    RW = D + 2
    assert ITEMS == TURNS * U and TILES == GROUPS * GT and ITEMS + U <= BLK * P and U % AGB == 0
    assert H == 512 and D == 256 and E == 8 and ETAIL > 0 and TAIL > 0 and EFULL == CHUNKS - 1
    assert BLOCKS == BTURNS * UB and TURNS + 1 <= P and BLOCKS <= 64

    with ExitStack() as ctx:
        def sb(name, shape, dt=F32):
            return ctx.enter_context(nc.sbuf_tensor(name, shape, dt))

        s = {}

        def S(name):
            if name not in s:
                s[name] = ctx.enter_context(nc.semaphore(name))
            return s[name]

        xn_d = nc.dram_tensor("xn_d", [NP, D], F32).ap()
        h_d = nc.dram_tensor("h_d", [NP, H], F32).ap()
        edges_d = nc.dram_tensor("edges_d", [CHUNKS + 1, 2 * P], I32).ap()
        tables_d = nc.dram_tensor("tables_d", [(BLK + 2) * P], I32).ap()
        rows_d = nc.dram_tensor("rows_d", [BLOCKS * P, RW], F32).ap()
        y_d = nc.dram_tensor("y_d", [2 * NP + BLOCKS * P, D], F32).ap()

        xs = sb("xs", [P, TILES, D])
        early = sb("early", [P, TILES * D + KD * H + KH * H])
        acc1 = early[:, 0:TILES * D].rearrange("p (t d) -> p t d", t=TILES)
        w1a = early[:, TILES * D:TILES * D + KD * H].rearrange("p (k n) -> p k n", k=KD)
        w1b = early[:, TILES * D + KD * H:TILES * D + (KD + KH) * H].rearrange("p (k n) -> p k n", k=KH)
        we1 = early[:, 0:E * KD * H].rearrange("p (e k n) -> p e k n", e=E, k=KD)
        late = sb("late", [P, TILES * H])
        acc2 = late[:, :].rearrange("p (t d) -> p t d", t=TILES)
        dst_i = late[0:EP, 0:EC].bitcast(I32)
        dst_f = late[0:EP, EC:2 * EC]
        below = [late[0:EP, (t + 1) * EC:(t + 2) * EC] for t in range(TILES)]
        scratch = late[:, (TILES + 1) * EC:]
        item_cmp = scratch[:, 0:3 * BLK * TILES].rearrange("p (k b t) -> p k b t", k=3, b=BLK)
        per_tile = scratch[:, 3 * BLK * TILES:(3 * BLK + 6) * TILES].rearrange("p (k t) -> p k t", k=6)
        chunk_lo = scratch[:, (3 * BLK + 6) * TILES:(3 * BLK + 8) * TILES].rearrange("p (k t) -> p k t", k=2)
        rows = late[:, 0:TILES * RW].rearrange("p (t r) -> p t r", t=TILES)
        ys = late[:, :].rearrange("p (k t d) -> p k t d", k=2, t=TILES)
        ring = sb("ring", [P, U, H])
        flat = ring[:, :, :].rearrange("p u d -> p (u d)")
        item_edges_i = flat[:, 0:BLK * 2 * P].bitcast(I32).rearrange("p (b c) -> p b c", b=BLK)
        item_edges_f = flat[:, BLK * 2 * P:2 * BLK * 2 * P].rearrange("p (b c) -> p b c", b=BLK)
        xn2 = flat[:, 0:GT * D].rearrange("p (t d) -> p t d", t=GT)
        gT = flat[:, GT * D:GT * D + KD * GN].rearrange("p (k n) -> p k n", k=KD)
        o = 0
        xb = flat[:, o:o + UB * RW].rearrange("p (u r) -> p u r", u=UB); o += UB * RW
        yb = flat[:, o:o + UB * D].rearrange("p (u d) -> p u d", u=UB); o += UB * D
        xbT = flat[:, o:o + KD * P].rearrange("p (k n) -> p k n", k=KD); o += KD * P
        w_now = [flat[:, o + u * KD * H:o + (u + 1) * KD * H] for u in range(UB - 1)]; o += (UB - 1) * KD * H
        assert o <= U * H
        w2a_b2 = sb("w2a_b2", [P, KH * H])
        w2a = w2a_b2[:, :].rearrange("p (k n) -> p k n", k=KH)
        b2_all = w2a_b2[:, 0:E * D].rearrange("p (e d) -> p e d", e=E)
        w2b = sb("w2b", [P, KH, D])
        we2 = sb("we2", [P, E, KH, D])
        wg = sb("wg", [P, KD, E])
        b1a_c = sb("b1a_c", [P, KH])
        b2a_c = sb("b2a_c", [P, KH])
        b1_c = sb("b1_c", [P, E, KH])
        b1b_r = sb("b1b_r", [1, H])
        b2b_r = sb("b2b_r", [1, D])
        bg_r = sb("bg_r", [1, E])
        scale1 = sb("scale1", [P, 1])
        scale2 = sb("scale2", [P, 1])
        ident = sb("ident", [P, P])
        ones = sb("ones", [P, P])
        before = sb("before", [P, P])
        node_id = sb("node_id", [P, P])
        item_id = sb("item_id", [P, BLK])
        turn_id = sb("turn_id", [P, 2])
        expert_id = sb("expert_id", [P, TILES, E])
        block_row = sb("block_row", [P, BLOCKS])
        pad_rows = sb("pad_rows", [2, 2 * P], I32)
        fill = sb("fill", [P, RW])
        cnt = sb("cnt", [P, TILES])
        bound = sb("bound", [P, TILES + 1])
        bound_i = sb("bound_i", [P, 2, TILES + 1], I32)
        item_sum = sb("item_sum", [P, 5, BLK])
        item_chunk_i = sb("item_chunk_i", [P, BLK], I32)
        tables_c = sb("tables_c", [P, BLK + 2], I32)
        tables = sb("tables", [1, (BLK + 2) * P], I32)
        tile_end_i = sb("tile_end_i", [P, TILES], I32)
        idx = sb("idx", [P, U], I32)
        work = sb("work", [P, 2 * BLK * P + U * P])
        src_col = work[:, 0:BLK * P].bitcast(I32)
        dst_col = work[:, BLK * P:2 * BLK * P]
        onehot = work[:, 2 * BLK * P:].rearrange("p (u n) -> p u n", u=U)
        parts = [work[:, k * TILES * E:(k + 1) * TILES * E].rearrange("p (t e) -> p t e", e=E) for k in range(9)]
        gates, top, first, second, either, at, total, upto = parts[0:8]
        top_i = work[:, 8 * TILES * E:9 * TILES * E].bitcast(mybir.dt.uint32).rearrange("p (t e) -> p t e", e=E)
        slot = work[:, 9 * TILES * E:9 * TILES * E + 2 * TILES].rearrange("p (k t) -> p k t", k=2)
        slot_i = work[:, 9 * TILES * E + 2 * TILES:9 * TILES * E + 4 * TILES].bitcast(I32).rearrange("p (k t) -> p k t", k=2)
        stats = sb("stats", [P, TILES, 6])
        mv = sb("mv", [P, TILES, 2])
        ln = sb("ln", [P, 5, TILES])
        stage = sb("stage", [P, H])
        aT = sb("aT", [P, KH, P])
        hT = sb("hT", [P, KH, P])
        hb = sb("hb", [P, 2, H])
        w_now.append(hb[:, :, :].rearrange("p j n -> p (j n)"))
        w_now = [w.rearrange("p (k n) -> p k n", k=KD) for w in w_now]
        hbT = [hT[:, :, :], aT[:, :, :], stage[:, :].rearrange("p (k n) -> p k n", k=KH)]
        per_expert = sb("per_expert", [P, 5, E])
        blocks_i = sb("blocks_i", [P, E], I32)
        block_expert = sb("block_expert", [P, 2, BLOCKS])
        block_expert_i = sb("block_expert_i", [P, BLOCKS], I32)
        dest = sb("dest", [P, 3, BLOCKS])
        dest_i = sb("dest_i", [P, UB], I32)

        bank = [ctx.enter_context(nc.psum_tensor(f"bank{i}", [P, 512], F32)) for i in range(8)]

        NWEIGHTS = 13
        x_in, edges_in, pad_made, pad_put, dst_in, fill_put = (
            S("x_in"), S("edges_in"), S("pad_made"), S("pad_put"), S("dst_in"), S("fill_put"))
        consts, weights_in, prep, cnt_sum = S("consts"), S("weights_in"), S("prep"), S("cnt_sum")
        chunk_ids, items_in, items_T, tables_out, tables_in = (
            S("chunk_ids"), S("items_in"), S("items_T"), S("tables_out"), S("tables_in"))
        cols_made, tables_made = S("cols_made"), S("tables_made")
        stats_made, var_made, root_made, xn_made, xn_put = (
            S("stats_made"), S("var_made"), S("root_made"), S("xn_made"), S("xn_put"))
        scaled = S("scaled")
        gathered = [[S(f"gathered{L}_{u}") for u in range(U)] for L in range(2)]
        item_ready = [S(f"item_ready{L}") for L in range(2)]
        item_summed = [S(f"item_summed{L}") for L in range(2)]
        item_added = [S(f"item_added{L}") for L in range(2)]
        staged = [S(f"staged{L}") for L in range(2)]
        turned = [S(f"turned{L}") for L in range(2)]
        turned_out = [S(f"turned_out{L}") for L in range(2)]
        up = [S(f"up{L}") for L in range(2)]
        up_out = [S(f"up_out{L}") for L in range(2)]
        down = [S(f"down{L}") for L in range(2)]
        down_free = [S(f"down_free{L}") for L in range(2)]
        h_scaled = S("h_scaled")
        h_put = [S(f"h_put{j}") for j in range(2)]
        x2_var, x2_root, xn2_made, xn2_turned, xn2_out, gate_sum, gate_out, rows_made, xn2_copied = (
            S("x2_var"), S("x2_root"), S("xn2_made"), S("xn2_turned"), S("xn2_out"), S("gate_sum"), S("gate_out"),
            S("rows_made"), S("xn2_copied"))
        picked, placed, slots_made, blocks_made, scattered = (
            S("picked"), S("placed"), S("slots_made"), S("blocks_made"), S("scattered"))
        expert1_in, expert2_in, bias2_in = S("expert1_in"), S("expert2_in"), S("bias2_in")
        block_in = [S(f"block_in{u}") for u in range(UB)]
        bx_turned, bx_out, w_copied, bh, bg_out, by, by_out, dest_made = (
            S("bx_turned"), S("bx_out"), S("w_copied"), S("bh"), S("bg_out"), S("by"), S("by_out"), S("dest_made"))
        block_put = [S(f"block_put{u}") for u in range(UB)]
        ys_in = [S(f"ys_in{g}") for g in range(GROUPS)]
        first_added, summed, out_put = S("first_added"), S("summed"), S("out_put")
        dve = S("dve")

        def tile(a, t, n=1):
            return a[:, ds(t, n), :].rearrange("p t d -> p (t d)")

        block = ctx.enter_context(nc.Block())

        @block.sync
        def _(sp):
            sp.dma_start(dst_i, dst.rearrange("(p c) -> p c", p=EP)).then_inc(dst_in, 16)
            sp.dma_start(xs[:, 0:FULL, :], x[0:FULL * P, :].rearrange("(t p) d -> p t d", p=P)).then_inc(x_in, 16)
            sp.wait_ge(pad_made, 3)
            sp.dma_start(xs[0:TAIL, FULL, :], x[FULL * P:N, :]).then_inc(x_in, 16)
            sp.dma_start(edges_d[CHUNKS - 1:CHUNKS + 1, :], pad_rows[:, :]).then_inc(pad_put, 16)
            for c, a in enumerate((src, dst)):
                sp.dma_start(edges_d[0:EFULL, c * P:c * P + P],
                             a[0:EFULL * P].rearrange("(c e) -> c e", e=P)).then_inc(edges_in, 16)
            sp.wait_ge(pad_put, 16)
            for c, a in enumerate((src, dst)):
                sp.dma_start(edges_d[EFULL:EFULL + 1, c * P:c * P + ETAIL],
                             a[EFULL * P:EDGES].rearrange("(c e) -> c e", c=1)).then_inc(edges_in, 16)
            with nc.allow_non_contiguous_dma(reason="biases as columns, one scalar for all partitions"):
                sp.dma_start(scale1[:, :], eps1.rearrange("(a b) -> a b", a=1).to_broadcast([P, 1])).then_inc(weights_in, 16)
                sp.dma_start(scale2[:, :], eps2.rearrange("(a b) -> a b", a=1).to_broadcast([P, 1])).then_inc(weights_in, 16)
                sp.wait_ge(tables_made, 1)
                sp.dma_start(tables_d.rearrange("(b p) -> p b", p=P), tables_c[:, :]).then_inc(tables_out, 16)
                sp.wait_ge(tables_out, 16)
                sp.dma_start(tables[:, :], tables_d.rearrange("(a n) -> a n", a=1)).then_inc(tables_in, 16)
                sp.wait_ge(xn_made, TILES)
                sp.dma_start(xn_d.rearrange("(t p) d -> p t d", p=P), acc1).then_inc(xn_put, 16)
                loads = [
                    (w1a, W1a.rearrange("(k p) n -> p k n", p=P)),
                    (w1b, W1b.rearrange("(k p) n -> p k n", p=P)),
                    (w2a, W2a.rearrange("(k p) n -> p k n", p=P)),
                    (w2b[:, :, :], W2b.rearrange("(k p) n -> p k n", p=P)),
                    (wg[:, :, :], Wg.rearrange("(k p) n -> p k n", p=P)),
                    (b1a_c[:, :], b1a.rearrange("(k p) -> p k", p=P)),
                    (b2a_c[:, :], b2a.rearrange("(k p) -> p k", p=P)),
                    (b1_c[:, :, :], b1.rearrange("e (k p) -> p e k", p=P)),
                    (b1b_r[:, :], b1b.rearrange("(a n) -> a n", a=1)),
                    (b2b_r[:, :], b2b.rearrange("(a n) -> a n", a=1)),
                    (bg_r[:, :], bg.rearrange("(a n) -> a n", a=1)),
                ]
                assert len(loads) + 2 == NWEIGHTS
                for to, of in loads:
                    sp.dma_start(to, of).then_inc(weights_in, 16)
            sp.dma_start(rows_d.rearrange("(b p) r -> p b r", p=P),
                         fill[:, :].rearrange("p (o r) -> p o r", o=1).to_broadcast([P, BLOCKS, RW])).then_inc(fill_put, 16)
            sp.dma_start(we2[:, :, :, :].rearrange("p e k n -> p (e k) n"),
                         W2.rearrange("e (k p) n -> p (e k) n", p=P)).then_inc(expert2_in, 16)
            hd = h_d.rearrange("(t p) d -> t p d", p=P)

            def put_hidden(t, j):
                sp.wait_ge(down_free[0], t + 2)
                sp.dma_start(hd[ds(t, 1), :, :].rearrange("t p d -> (t p) d"), hb[:, j, :]).then_inc(h_put[j], 16)

            with sp.Fori(0, TILES - 1, 2) as t:
                put_hidden(t, 0)
                put_hidden(t + 1, 1)
            put_hidden(TILES - 1, 0)
            sp.wait_ge(down[0], TILES)
            sp.wait_ge(staged[0], TILES)
            sp.dma_start(we1.rearrange("p e k n -> p (e k) n"),
                         W1.rearrange("e (k p) n -> p (e k) n", p=P)).then_inc(expert1_in, 16)

            sp.wait_ge(down[1], TILES)
            sp.dma_start(w2a_b2[:, 0:E * D], b2.rearrange("e d -> (e d)").rearrange("(a n) -> a n", a=1)
                         .to_broadcast([P, E * D])).then_inc(bias2_in, 16)

            def load_block(b, u):
                sp.dma_start(xb[:, u, :], rows_d.rearrange("(b p) r -> b p r", p=P)[ds(b, 1), :, :]
                             .rearrange("b p r -> (b p) r")).then_inc(block_in[u], 16)
            sp.wait_ge(scattered, 16 * 2 * TILES)
            sp.wait_ge(fill_put, 16)
            for u in range(UB):
                load_block(u, u)
            with sp.Fori(1, BTURNS) as n:
                for u in range(UB):
                    sp.wait_ge(bx_turned, n * UB + (u + 1 - UB))
                    sp.wait_ge(dest_made, n * UB + (u + 1 - UB))
                    load_block(n * UB + u, u)
            for u in range(UB):
                sp.wait_ge(block_put[u], 16 * BTURNS)
            for g in range(GROUPS):
                for k in range(2):
                    r0 = k * NP + g * GN
                    sp.dma_start(ys[:, k, g * GT:g * GT + GT, :],
                                 y_d[r0:r0 + GN, :].rearrange("(t p) d -> p t d", p=P)).then_inc(ys_in[g], 16)
            for g in range(GROUPS):
                sp.wait_ge(summed, g + 1)
                t0, t1 = g * GT, min(g * GT + GT, FULL)
                sp.dma_start(out[t0 * P:t1 * P, :].rearrange("(t p) d -> p t d", p=P), xs[:, t0:t1, :]).then_inc(out_put, 16)
            sp.dma_start(out[FULL * P:N, :], xs[0:TAIL, FULL, :]).then_inc(out_put, 16)
            sp.wait_ge(out_put, 16 * (GROUPS + 1))

        @block.gpsimd
        def _(pool):
            pool.memset(pad_rows[:, 0:P], 0).then_inc(pad_made, 1)
            pool.memset(pad_rows[:, P:2 * P], -1).then_inc(pad_made, 1)
            pool.memset(xs[:, FULL, :], 0.0).then_inc(pad_made, 1)
            pool.memset(ones[:, :], 1.0).then_inc(consts, 1)
            pool.memset(ident[:, :], 0.0).then_inc(consts, 1)
            f32 = dict(allow_small_or_imprecise_dtypes=True)
            pool.iota(node_id[:, :], [[1, P]], base=0, channel_multiplier=0, **f32).then_inc(consts, 1)
            pool.iota(item_id[:, :], [[P, BLK]], base=0, channel_multiplier=1, **f32).then_inc(consts, 1)
            pool.iota(turn_id[:, 0:1], [[1, 1]], base=0, channel_multiplier=U, **f32).then_inc(consts, 1)
            pool.iota(expert_id[:, :, :], [[0, TILES], [1, E]], base=0, channel_multiplier=0, **f32).then_inc(consts, 1)
            pool.iota(block_row[:, :], [[P, BLOCKS]], base=0, channel_multiplier=0, **f32).then_inc(consts, 1)
            pool.memset(fill[:, 0:D], 0.0).then_inc(consts, 1)
            pool.iota(fill[:, D:D + 1], [[1, 1]], base=NP, channel_multiplier=1, **f32).then_inc(consts, 1)
            pool.memset(fill[:, D + 1:D + 2], -1.0).then_inc(consts, 1)
            pool.memset(stats[:, :, :], 0.0).then_inc(down_free[0], 1)
            pool.memset(mv[:, :, :], 0.0).then_inc(down_free[1], 1)
            pool.wait_ge(consts, 10)
            pool.affine_select(out=ident[:, :], in_=ident[:, :], compare_op=ALU.not_equal, fill=1.0,
                               base=0, pattern=[[-1, P]], channel_multiplier=1).then_inc(consts, 1)
            pool.affine_select(out=before[:, :], in_=ones[:, :], compare_op=ALU.is_gt, fill=0.0,
                               base=0, pattern=[[1, P]], channel_multiplier=-1).then_inc(consts, 1)
            pool.wait_ge(edges_in, 64)
            pool.wait_ge(pad_put, 16)
            pool.wait_ge(chunk_ids, 1)
            for b in range(BLK):
                pool.indirect_dma_start(item_edges_i[:, b, :], None, edges_d[:, :],
                                        bass.IndirectOffsetOnAxis(item_chunk_i[:, b:b + 1], 0)).then_inc(items_in, 16)

            def gathers(L):
                table, W = ((xn_d, D), (h_d, H))[L]
                with pool.Fori(0, TURNS) as n:
                    for u in range(U):
                        if u % GG == 0:
                            pool.wait_ge(item_ready[L], n * U + (u + GG))
                            pool.nop(nofuse=True)
                        pool.indirect_dma_start(ring[:, u, 0:W], None, table[:, :],
                                                bass.IndirectOffsetOnAxis(idx[:, u:u + 1], 0)).then_inc(gathered[L][u], 16)

            pool.wait_ge(xn_put, 16)
            gathers(0)
            for j in range(2):
                pool.wait_ge(h_put[j], 16 * ((TILES + 1 - j) // 2))
            gathers(1)
            pool.wait_ge(staged[1], TILES)
            pool.iota(rows[:, :, D:D + 1], [[P, TILES], [0, 1]], base=0, channel_multiplier=1, **f32).then_inc(rows_made, 1)
            with pool.Fori(0, GROUPS) as g:
                pool.wait_ge(xn2_made, g + 1)
                pool.tensor_copy(rows[:, ds(g * GT, GT), 0:D], xn2).then_inc(xn2_copied, 1)
            pool.wait_ge(slots_made, 1)
            pool.wait_ge(rows_made, 2)
            pool.wait_ge(xn2_copied, GROUPS)
            pool.wait_ge(fill_put, 16)
            for t in range(TILES):
                for k in range(2):
                    pool.indirect_dma_start(rows_d[:, :], bass.IndirectOffsetOnAxis(slot_i[:, k, t:t + 1], 0),
                                            rows[:, t, :], None).then_inc(scattered, 16)
            with pool.Fori(0, BTURNS) as n:
                for u in range(UB):
                    pool.wait_ge(by_out, n * UB + (u + 1))
                    pool.nop(nofuse=True)
                    pool.indirect_dma_start(y_d[:, :], bass.IndirectOffsetOnAxis(dest_i[:, u:u + 1], 0),
                                            yb[:, u, :], None).then_inc(block_put[u], 16)

        @block.scalar
        def _(act):
            act.wait_ge(var_made, 1)
            act.activation(ln[:, 1, :], ln[:, 0, :], ACT.Sqrt).then_inc(root_made, 1)
            act.wait_ge(weights_in, 16 * NWEIGHTS)
            act.wait_ge(scaled, 2)
            act.wait_ge(tables_in, 16)

            def stage_tile(L, t, first):
                acc, W = ((acc1, D), (acc2, H))[L]
                end = act.value_load(tables[0:1, ds(t + (BLK + 1) * P, 1)], min_val=1, max_val=ITEMS)
                act.wait_ge(item_added[L], end)
                if not first:
                    act.wait_ge(turned[L], t)
                act.copy(stage[:, 0:W], tile(acc, t)).then_inc(staged[L], 1)

            def mlp(L, t):
                K = (KD, KH)[L]
                bias = (b1a_c, b2a_c)[L]
                act.wait_ge(turned[L], t + 1)
                act.copy(aT[:, 0:K, :], bank[3][:, 0:K * P].rearrange("p (k n) -> p k n", k=K)).then_inc(turned_out[L], 1)
                for m in range(KH):
                    act.wait_ge(up[L], t * 2 + (1 + m // 2))
                    act.activation(hT[:, m, :], bank[4 + m // 2][:, (m % 2) * P:(m % 2) * P + P], ACT.Relu,
                                   bias=bias[:, m:m + 1]).then_inc(up_out[L], 1)

            def hidden(t, j, first):
                mlp(0, t)
                act.wait_ge(down[0], t + 1)
                if not first:
                    act.wait_ge(h_put[j], (t - j) * 8)
                    act.wait_ge(h_scaled, t - 1)
                act.activation(hb[:, j, :], bank[6][:, :], ACT.Relu).then_inc(down_free[0], 1)
                act.wait_ge(down_free[0], t + 2)
                act.activation(tile(acc2, t), hb[:, j, :], ACT.Copy, scale=scale2[:, :]).then_inc(h_scaled, 1)

            stage_tile(0, 0, True)
            hidden(0, 0, True)
            stage_tile(0, 1, False)
            hidden(1, 1, True)
            with act.Fori(2, TILES - 1, 2) as t:
                for j in range(2):
                    stage_tile(0, t + j, False)
                    hidden(t + j, j, False)
            stage_tile(0, TILES - 1, False)
            hidden(TILES - 1, 0, False)

            def residual(t):
                mlp(1, t)
                act.wait_ge(down[1], t + 1)
                act.copy(tile(xs, t), bank[6][:, 0:D]).then_inc(down_free[1], 1)

            stage_tile(1, 0, True)
            residual(0)
            with act.Fori(1, TILES) as t:
                stage_tile(1, t, False)
                residual(t)
            act.wait_ge(x2_var, 1)
            act.activation(ln[:, 1, :], ln[:, 0, :], ACT.Sqrt).then_inc(x2_root, 1)
            with act.Fori(0, GROUPS) as g:
                for j in range(GT):
                    act.wait_ge(xn2_turned, g * GT + (j + 1))
                    act.copy(gT[:, :, j * P:j * P + P],
                             bank[3 + j % 2][:, 0:KD * P].rearrange("p (k n) -> p k n", k=KD)).then_inc(xn2_out, 1)

            def take_x(i):
                act.wait_ge(bx_turned, i + 1)
                act.copy(xbT, bank[3][:, 0:KD * P].rearrange("p (k n) -> p k n", k=KD)).then_inc(bx_out, 1)

            def gelu(i, u, first):
                e = act.value_load(block_expert_i[0:1, ds(i, 1)], min_val=0, max_val=E - 1)
                act.wait_ge(bh, i + 1)
                if not first:
                    act.wait_ge(by, i - 2)
                act.nop(nofuse=True)
                for k in range(KH):
                    act.activation(hbT[u][:, k, :], bank[u][:, k * P:k * P + P], ACT.Gelu,
                                   bias=b1_c[:, ds(e, 1), k:k + 1].rearrange("p e k -> p (e k)")).then_inc(bg_out, 1)

            act.wait_ge(blocks_made, 1)
            take_x(0)
            take_x(1)
            gelu(0, 0, True)
            for v in range(UB):
                take_x(v + 2)
                gelu(v + 1, (v + 1) % UB, v + 1 < UB)
            with act.Fori(1, BTURNS - 1) as n:
                for v in range(UB):
                    take_x(n * UB + (v + 2))
                    gelu(n * UB + (v + 1), (v + 1) % UB, False)
            take_x(BLOCKS - 1)
            gelu(BLOCKS - 2, 1, False)
            gelu(BLOCKS - 1, 2, False)

        @block.tensor
        def _(pe):
            pe.wait_ge(consts, 12)
            pe.wait_ge(prep, 1)
            pe.matmul(bank[0][:, 0:TILES - 1], ones[0:EP, :], cnt[0:EP, 0:TILES - 1], start=True, stop=True).then_inc(cnt_sum, 1)
            pe.wait_ge(prep, 2)
            for b in range(BLK):
                for c in range(2):
                    pe.transpose(bank[1 + c][:, b * P:b * P + P], item_edges_f[:, b, c * P:c * P + P],
                                 ident[:, :]).then_inc(items_T, 1)

            def sum_item(L, n, u, first):
                W = (D, H)[L]
                i1 = n * U + (u + 1)
                pe.wait_ge(item_ready[L], i1)
                if not (first and u < AGB):
                    pe.wait_ge(item_added[L], i1 - AGB)
                pe.wait_ge(gathered[L][u], n * 16 + 16)
                pe.matmul(bank[u % AGB][:, 0:W], onehot[:, u, :], ring[:, u, 0:W],
                          start=True, stop=True).then_inc(item_summed[L], 1)

            def turn_tile(L, t):
                pe.wait_ge(staged[L], t + 1)
                for k in range((KD, KH)[L]):
                    mm = pe.transpose(bank[3][:, k * P:k * P + P], stage[:, k * P:k * P + P], ident[:, :])
                mm.then_inc(turned[L], 1)

            def up_product(L, t, half):
                K, w = ((KD, w1a), (KH, w2a))[L]
                if half == 0:
                    pe.wait_ge(turned_out[L], t + 1)
                for m in (2 * half, 2 * half + 1):
                    for k in range(K):
                        mm = pe.matmul(bank[4 + half][:, (m % 2) * P:(m % 2) * P + P], w[:, k, m * P:m * P + P],
                                       aT[:, k, :], start=(k == 0), stop=(k == K - 1))
                mm.then_inc(up[L], 1)

            def down_product(L, t, half):
                wd, row, W = ((w1b, b1b_r, H), (w2b, b2b_r, D))[L]
                if half == 0:
                    pe.wait_ge(down_free[L], t + 1)
                    pe.matmul(bank[6][:, 0:W], ones[0:1, :], row[:, :], start=True, stop=False)
                    if L == 1:
                        pe.matmul(bank[6][:, 0:W], ident[:, :], tile(xs, t), start=False, stop=False)
                for k in (2 * half, 2 * half + 1):
                    pe.wait_ge(up_out[L], t * KH + (k + 1))
                    mm = pe.matmul(bank[6][:, 0:W], hT[:, k, :], wd[:, k, :], start=False, stop=(k == KH - 1))
                if half == 1:
                    mm.then_inc(down[L], 1)

            def dense(L, t):
                turn_tile(L, t)
                for half in range(2):
                    up_product(L, t, half)
                for half in range(2):
                    down_product(L, t, half)

            def complete_tiles(L, lo, hi):
                with pe.If(lo < hi):
                    with pe.Fori(lo, hi) as t:
                        dense(L, t)

            def turn(L, n):
                lo = pe.value_load(tables[0:1, ds(n + (BLK * P - 1), 1)], min_val=0, max_val=TILES - 1)
                hi = pe.value_load(tables[0:1, ds(n + BLK * P, 1)], min_val=0, max_val=TILES - 1)
                with pe.If(lo < hi):
                    for u in range(U):
                        sum_item(L, n, u, False)
                        if u == 0:
                            turn_tile(L, lo)
                        elif u in (2, 3):
                            up_product(L, lo, u - 2)
                        elif u in (5, 6):
                            down_product(L, lo, u - 5)
                    complete_tiles(L, lo + 1, hi)
                with pe.Else():
                    for u in range(U):
                        sum_item(L, n, u, False)

            pe.wait_ge(weights_in, 16 * NWEIGHTS)
            pe.wait_ge(tables_in, 16)
            for L in range(2):
                for u in range(U):
                    sum_item(L, 0, u, True)
                with pe.Fori(1, TURNS) as n:
                    turn(L, n)
                done = pe.value_load(tables[0:1, BLK * P + TURNS - 1:BLK * P + TURNS], min_val=0, max_val=TILES - 1)
                with pe.Fori(done, TILES) as t:
                    dense(L, t)

            with pe.Fori(0, GROUPS) as g:
                pe.wait_ge(xn2_made, g + 1)
                for j in range(GT):
                    if j >= 2:
                        pe.wait_ge(xn2_out, g * GT + (j - 1))
                    for k in range(KD):
                        mm = pe.transpose(bank[3 + j % 2][:, k * P:k * P + P], xn2[:, j, k * P:k * P + P], ident[:, :])
                    mm.then_inc(xn2_turned, 1)
                for j in range(GT):
                    pe.wait_ge(xn2_out, g * GT + (j + 1))
                    for k in range(KD):
                        pe.matmul(bank[6][:, j * E:j * E + E], gT[:, k, j * P:j * P + P], wg[:, k, :],
                                  start=(k == 0), stop=False)
                    mm = pe.matmul(bank[6][:, j * E:j * E + E], ones[0:1, :], bg_r[:, :], start=False, stop=True)
                mm.then_inc(gate_sum, 1)
                pe.wait_ge(gate_out, g + 1)
            pe.wait_ge(picked, 1)
            chosen = either.rearrange("p t e -> p (t e)")
            pe.matmul(bank[0][:, 0:TILES * E], before[:, :], chosen, start=True, stop=True).then_inc(placed, 1)
            pe.matmul(bank[1][:, 0:TILES * E], ones[:, :], chosen, start=True, stop=True).then_inc(placed, 1)

            def turn_x(i, u, n):
                pe.wait_ge(block_in[u], n * 16 + 16)
                for k in range(KD):
                    mm = pe.transpose(bank[3][:, k * P:k * P + P], xb[:, u, k * P:k * P + P], ident[:, :])
                mm.then_inc(bx_turned, 1)

            def first_product(i, u, first):
                pe.wait_ge(bx_out, i + 1)
                pe.wait_ge(w_copied, i + 1)
                if not first:
                    pe.wait_ge(bg_out, (i - 2) * KH)
                for m in range(KH):
                    for k in range(KD):
                        mm = pe.matmul(bank[u][:, m * P:m * P + P], w_now[u][:, k, m * P:m * P + P], xbT[:, k, :],
                                       start=(k == 0), stop=(k == KD - 1))
                mm.then_inc(bh, 1)

            def second_product(i, u, first):
                e = pe.value_load(block_expert_i[0:1, ds(i, 1)], min_val=0, max_val=E - 1)
                if not first:
                    pe.wait_ge(by_out, i - 2)
                for k in range(KH):
                    pe.wait_ge(bg_out, i * KH + (k + 1))
                    mm = pe.matmul(bank[5 + u][:, 0:D], hbT[u][:, k, :], we2[:, ds(e, 1), k, :].rearrange("p e n -> p (e n)"),
                                   start=(k == 0), stop=(k == KH - 1))
                mm.then_inc(by, 1)

            def step(n, v, first):
                i = n * UB + v
                first_product(i + 1, (v + 1) % UB, first and v + 1 < UB)
                turn_x(i + 2, (v + 2) % UB, n + (v + 2) // UB)
                second_product(i, v, first)

            pe.wait_ge(blocks_made, 1)
            pe.wait_ge(expert2_in, 16)
            turn_x(0, 0, 0)
            first_product(0, 0, True)
            turn_x(1, 1, 0)
            for v in range(UB):
                step(0, v, True)
            with pe.Fori(1, BTURNS - 1) as n:
                for v in range(UB):
                    step(n, v, False)
            step(BTURNS - 1, 0, False)
            first_product(BLOCKS - 1, 2, False)
            second_product(BLOCKS - 2, 1, False)
            second_product(BLOCKS - 1, 2, False)

        @block.vector
        def _(v):
            made = [0]

            def then(ins):
                made[0] += 1
                ins.then_inc(dve, 1)
                v.wait_ge(dve, made[0])

            v.wait_ge(dst_in, 16)
            then(v.tensor_copy(dst_f, dst_i))
            for t in range(1, TILES):
                ins = v.tensor_scalar(below[t], dst_f, float(t * P), None, ALU.is_lt, ALU.add, accum_out=cnt[0:EP, t - 1:t])
            ins.then_inc(prep, 1)
            v.memset(bound[:, 0:1], 0.0)
            v.memset(bound[:, TILES:TILES + 1], float(EDGES))
            v.wait_ge(consts, 12)
            v.tensor_scalar(turn_id[:, 1:2], turn_id[:, 0:1], 0.0, -1.0, ALU.is_equal, ALU.mult)
            v.wait_ge(cnt_sum, 1)
            then(v.tensor_copy(bound[:, 1:TILES], bank[0][:, 0:TILES - 1]))
            v.tensor_copy(bound_i[:, 0, :], bound[:, :])
            v.tensor_tensor(turn_id[:, 0:1], turn_id[:, 0:1], turn_id[:, 1:2], ALU.add)
            then(v.tensor_scalar(bound_i[:, 1, :], bound[:, :], float(P - 1), None, ALU.add))
            then(v.tensor_scalar(bound_i[:, :, :], bound_i[:, :, :], 7, None, ALU.arith_shift_right))
            v.tensor_copy(chunk_lo[:, 0, :], bound_i[:, 0, 0:TILES])
            then(v.tensor_copy(chunk_lo[:, 1, :], bound_i[:, 1, 1:TILES + 1]))
            n_, end_, start_, off_, step_, wait_ = (per_tile[:, k, :] for k in range(6))
            then(v.tensor_tensor(n_, chunk_lo[:, 1, :], chunk_lo[:, 0, :], ALU.subtract))
            then(v.tensor_tensor_scan(end_, n_, n_, 0.0, ALU.add, ALU.bypass))
            v.tensor_scalar(wait_[:, 0:TILES - 1], end_[:, 0:TILES - 1], 1.0, None, ALU.max)
            v.memset(wait_[:, TILES - 1:TILES], float(ITEMS))
            then(v.tensor_tensor(start_, end_, n_, ALU.subtract))
            then(v.tensor_tensor(off_, chunk_lo[:, 0, :], start_, ALU.subtract))
            then(v.tensor_tensor(step_[:, 1:TILES], off_[:, 1:TILES], off_[:, 0:TILES - 1], ALU.subtract))
            for b in range(BLK):
                v.tensor_scalar(item_cmp[:, 0, b, 1:TILES], start_[:, 1:TILES], item_id[:, b:b + 1], None, ALU.is_le)
                ins = v.scalar_tensor_tensor(out=item_cmp[:, 1, b, 1:TILES], in0=start_[:, 1:TILES], scalar=item_id[:, b:b + 1],
                                             in1=step_[:, 1:TILES], op0=ALU.is_le, op1=ALU.mult)
            v.tensor_scalar(item_cmp[:, 2, 0, :], wait_, turn_id[:, 0:1], None, ALU.is_le)
            then(v.tensor_tensor(item_cmp[:, 2, 1, :], wait_, ident[:, 0:TILES], ALU.mult))
            tile_, jump_, past_, chunk_, first_node = (item_sum[:, k, :] for k in range(5))
            v.tensor_reduce(tile_, item_cmp[:, 0, :, 1:TILES], AX_X, ALU.add)
            v.tensor_reduce(jump_, item_cmp[:, 1, :, 1:TILES], AX_X, ALU.add)
            v.tensor_reduce(bound[:, 0:2], item_cmp[:, 2, 0:2, :], AX_X, ALU.add)
            then(v.tensor_scalar(past_, item_id[:, :], end_[:, TILES - 1:TILES], float(2 * CHUNKS), ALU.is_ge, ALU.mult))
            v.tensor_copy(tables_c[:, BLK:BLK + 2], bound[:, 0:2])
            v.tensor_copy(tables_c[:, 0:BLK], tile_).then_inc(tables_made, 1)
            then(v.tensor_tensor(chunk_, item_id[:, :], jump_, ALU.add))
            then(v.tensor_tensor(chunk_, chunk_, past_, ALU.add))
            v.tensor_scalar(item_chunk_i[:, :], chunk_, float(CHUNKS), None, ALU.min).then_inc(chunk_ids, 1)
            then(v.tensor_scalar(first_node, tile_, float(P), None, ALU.mult))

            def statistics(made_sem, sources, base):
                with v.Fori(0, TILES) as t:
                    v.bn_stats(tile(stats, t), tile(sources, t)).then_inc(made_sem, 1)
                v.wait_ge(made_sem, base + TILES)

            def rstd_of(roots, made_sem):
                veps, root, rec, quo, rstd = (ln[:, k, :] for k in range(5))
                mean, half_gap = mv[:, :, 0], mv[:, :, 1]
                st = [stats[:, :, k] for k in range(6)]
                v.tensor_tensor(mean, st[1], st[4], ALU.add)
                v.tensor_tensor(half_gap, st[1], st[4], ALU.subtract)
                then(v.tensor_tensor(veps, st[2], st[5], ALU.add))
                v.tensor_scalar(mean, mean, 0.5, None, ALU.mult)
                then(v.tensor_scalar(half_gap, half_gap, 0.5, None, ALU.mult))
                v.tensor_scalar(veps, veps, 1.0 / D, LN_EPS, ALU.mult, ALU.add)
                then(v.tensor_tensor(half_gap, half_gap, half_gap, ALU.mult))
                v.tensor_tensor(veps, veps, half_gap, ALU.add).then_inc(made_sem, 1)
                v.wait_ge(roots, 1)
                then(v.reciprocal(rec, root))
                then(v.tensor_tensor(quo, veps, rec, ALU.mult))
                then(v.tensor_tensor(quo, quo, root, ALU.add))
                then(v.tensor_scalar(quo, quo, 0.5, None, ALU.mult))
                then(v.reciprocal(rstd, quo))

            v.wait_ge(x_in, 32)
            v.wait_ge(down_free[0], 1)
            v.wait_ge(down_free[1], 1)
            statistics(stats_made, xs, 0)
            rstd_of(root_made, var_made)
            with v.Fori(0, TILES) as t:
                v.tensor_scalar(tile(acc1, t), tile(xs, t), mv[:, ds(t, 1), 0:1].rearrange("p t d -> p (t d)"),
                                ln[:, 4, ds(t, 1)], ALU.subtract, ALU.mult).then_inc(xn_made, 1)
            v.wait_ge(items_in, 16 * BLK)
            v.tensor_copy(item_edges_f[:, :, 0:P], item_edges_i[:, :, 0:P])
            for b in range(BLK):
                ins = v.tensor_scalar(item_edges_f[:, b, P:2 * P], item_edges_i[:, b, P:2 * P], first_node[:, b:b + 1], None,
                                      ALU.subtract)
            ins.then_inc(prep, 1)
            v.wait_ge(items_T, 2 * BLK)
            v.tensor_copy(src_col, bank[1][:, :]).then_inc(cols_made, 1)
            v.tensor_copy(dst_col, bank[2][:, :]).then_inc(cols_made, 1)
            v.wait_ge(weights_in, 32)

            def item(L, i, u):
                v.tensor_copy(idx[:, u:u + 1], src_col[:, ds(i, 1)])
                v.tensor_scalar(onehot[:, u, :], node_id[:, :], dst_col[:, ds(i, 1)], None,
                                ALU.is_equal).then_inc(item_ready[L], 1)

            def first_items(L):
                for u in range(U):
                    item(L, u, u)

            def add_items(L):
                acc, W = ((acc1, D), (acc2, H))[L]
                with v.Fori(0, TURNS) as n:
                    for u in range(U):
                        i = n * U + u
                        t = v.value_load(tables[0:1, ds(i, 1)], min_val=0, max_val=TILES - 1)
                        v.wait_ge(item_ready[L], i + U)
                        v.wait_ge(item_summed[L], i + 1)
                        v.tensor_tensor(tile(acc, t), tile(acc, t), bank[u % AGB][:, 0:W], ALU.add).then_inc(item_added[L], 1)
                        item(L, i + U, u)

            v.wait_ge(cols_made, 2)
            first_items(0)
            v.tensor_scalar(scale1[:, :], scale1[:, :], 1.0, None, ALU.add).then_inc(scaled, 1)
            v.tensor_scalar(scale2[:, :], scale2[:, :], 1.0, None, ALU.add).then_inc(scaled, 1)
            v.wait_ge(scaled, 2)
            v.wait_ge(xn_put, 16)
            then(v.tensor_scalar(acc1, acc1, scale1[:, :], None, ALU.mult))
            v.wait_ge(tables_in, 16)
            add_items(0)
            v.wait_ge(item_ready[0], ITEMS + U)
            for u in range(U):
                v.wait_ge(gathered[0][u], 16 * TURNS)
            first_items(1)
            v.wait_ge(h_scaled, TILES)
            add_items(1)

            v.wait_ge(down_free[1], TILES + 1)
            statistics(stats_made, xs, TILES)
            rstd_of(x2_root, x2_var)
            def norm_group(g, first):
                if not first:
                    v.wait_ge(xn2_turned, g * GT)
                    v.wait_ge(xn2_copied, g)
                for j in range(GT):
                    ins = v.tensor_scalar(xn2[:, j, :], tile(xs, g * GT + j),
                                          mv[:, ds(g * GT + j, 1), 0:1].rearrange("p t d -> p (t d)"),
                                          ln[:, 4, ds(g * GT + j, 1)], ALU.subtract, ALU.mult)
                ins.then_inc(xn2_made, 1)
                v.wait_ge(gate_sum, g + 1)
                v.tensor_copy(gates[:, ds(g * GT, GT), :],
                              bank[6][:, 0:GT * E].rearrange("p (t e) -> p t e", e=E)).then_inc(gate_out, 1)

            norm_group(0, True)
            with v.Fori(1, GROUPS) as g:
                norm_group(g, False)
            v.wait_ge(gate_out, GROUPS)
            for t in range(TILES):
                ins = v.max(top[:, t, :], gates[:, t, :])
            then(ins)
            for t in range(TILES):
                ins = v.max_index(top_i[:, t, :], top[:, t, :], gates[:, t, :])
            then(ins)
            then(v.tensor_copy(top, top_i))
            v.wait_ge(staged[1], TILES)
            v.tensor_copy(rows[:, :, D + 1:D + 2], top[:, :, 0:1]).then_inc(rows_made, 1)
            for k, pick in enumerate((first, second)):
                ins = v.tensor_tensor(pick, expert_id[:, :, :], top[:, :, k:k + 1].to_broadcast([P, TILES, E]),
                                      ALU.is_equal)
            then(ins)
            v.tensor_tensor(either, first, second, ALU.add).then_inc(picked, 1)
            v.wait_ge(placed, 2)
            n_e, blocks_e, end_e, start_e, base_e = (per_expert[:, k, :] for k in range(5))
            v.tensor_copy(at, bank[0][:, 0:TILES * E].rearrange("p (t e) -> p t e", e=E))
            then(v.tensor_copy(total, bank[1][:, 0:TILES * E].rearrange("p (t e) -> p t e", e=E)))
            for e in range(E):
                ins = v.tensor_tensor_scan(upto[:, :, e], total[:, :, e], total[:, :, e], 0.0, ALU.add, ALU.bypass)
            then(ins)
            v.tensor_tensor(at, at, total, ALU.subtract)
            then(v.tensor_scalar(blocks_i[:, :], upto[:, TILES - 1, :], float(P - 1), None, ALU.add))
            then(v.tensor_scalar(blocks_i[:, :], blocks_i[:, :], 7, None, ALU.arith_shift_right))
            then(v.tensor_copy(blocks_e, blocks_i[:, :]))
            v.tensor_tensor(at, at, upto, ALU.add)
            then(v.tensor_tensor_scan(end_e, blocks_e, blocks_e, 0.0, ALU.add, ALU.bypass))
            then(v.tensor_tensor(start_e, end_e, blocks_e, ALU.subtract))
            then(v.tensor_scalar(base_e, start_e, float(P), None, ALU.mult))
            then(v.tensor_tensor(at, at, base_e.rearrange("p (o e) -> p o e", o=1).to_broadcast([P, TILES, E]), ALU.add))
            for pick in (first, second):
                ins = v.tensor_tensor(pick, pick, at, ALU.mult)
            then(ins)
            for k, pick in enumerate((first, second)):
                ins = v.tensor_reduce(slot[:, k, :], pick, AX_X, ALU.add)
            then(ins)
            v.tensor_copy(slot_i, slot).then_inc(slots_made, 1)
            then(v.tensor_scalar(block_expert[:, 1, :], block_row[:, :], base_e[:, 1:2], None, ALU.is_ge))
            for e in range(2, E):
                a, b = (1, 0) if e % 2 == 0 else (0, 1)
                then(v.scalar_tensor_tensor(out=block_expert[:, b, :], in0=block_row[:, :], scalar=base_e[:, e:e + 1],
                                            in1=block_expert[:, a, :], op0=ALU.is_ge, op1=ALU.add))
            experts = block_expert[:, b, :]
            v.tensor_copy(block_expert_i[:, :], experts).then_inc(blocks_made, 1)
            v.wait_ge(blocks_made, 1)

            def prepare(i, u, n, first):
                v.wait_ge(block_in[u], n * 16 + 16)
                node, expert = xb[:, u, D:D + 1], xb[:, u, D + 1:D + 2]
                v.tensor_scalar(dest[:, 0, ds(i, 1)], expert, experts[:, ds(i, 1)], float(NP), ALU.not_equal, ALU.mult)
                v.scalar_tensor_tensor(out=dest[:, 1, ds(i, 1)], in0=expert, scalar=0.0, in1=block_row[:, ds(i, 1)],
                                       op0=ALU.is_lt, op1=ALU.mult)
                v.tensor_copy(dest[:, 2, ds(i, 1)], node).then_inc(dest_made, 1)
                e = v.value_load(block_expert_i[0:1, ds(i, 1)], min_val=0, max_val=E - 1)
                if not first:
                    v.wait_ge(bh, i - 2)
                v.tensor_copy(w_now[u], we1[:, ds(e, 1), :, :].rearrange("p e k n -> p (e k) n")).then_inc(w_copied, 1)

            def take_y(i, u, n, first):
                e = v.value_load(block_expert_i[0:1, ds(i, 1)], min_val=0, max_val=E - 1)
                v.wait_ge(dest_made, i + 1)
                if first:
                    v.wait_ge(bias2_in, 16)
                else:
                    v.wait_ge(block_put[u], n * 16)
                v.scalar_tensor_tensor(out=dest_i[:, u:u + 1], in0=dest[:, 0, ds(i, 1)], scalar=dest[:, 1, ds(i, 1)],
                                       in1=dest[:, 2, ds(i, 1)], op0=ALU.add, op1=ALU.add)
                v.wait_ge(by, i + 1)
                v.tensor_tensor(yb[:, u, :], bank[5 + u][:, 0:D], tile(b2_all, e), ALU.add).then_inc(by_out, 1)

            v.wait_ge(expert1_in, 16)
            for u in range(UB):
                prepare(u, u, 0, True)
            for u in range(UB):
                prepare(u + UB, u, 1, False)
                take_y(u, u, 0, True)
            with v.Fori(1, BTURNS - 1) as n:
                for u in range(UB):
                    prepare(n * UB + (u + UB), u, n + 1, False)
                    take_y(n * UB + u, u, n, False)
            for u in range(UB):
                take_y(BLOCKS - UB + u, u, BTURNS - 1, False)

            for g in range(GROUPS):
                ts = slice(g * GT, g * GT + GT)
                v.wait_ge(ys_in[g], 32)
                v.tensor_tensor(xs[:, ts, :], xs[:, ts, :], ys[:, 0, ts, :], ALU.add).then_inc(first_added, 1)
                v.wait_ge(first_added, g + 1)
                v.tensor_tensor(xs[:, ts, :], xs[:, ts, :], ys[:, 1, ts, :], ALU.add).then_inc(summed, 1)


_INS = ['x', 'src', 'dst', 'L0_gnn_W1a', 'L0_gnn_b1a', 'L0_gnn_W1b', 'L0_gnn_b1b', 'L0_gnn_W2a', 'L0_gnn_b2a',
        'L0_gnn_W2b', 'L0_gnn_b2b', 'L0_gnn_eps1', 'L0_gnn_eps2', 'L0_ffn_Wg', 'L0_ffn_bg', 'L0_ffn_W1', 'L0_ffn_b1',
        'L0_ffn_W2', 'L0_ffn_b2']


def kernel(**inputs):
    import numpy as _np
    import concourse.bacc as _bacc
    from concourse import mybir as _mybir
    from concourse.bass_utils import run_bass_kernel_spmd as _run

    nc = _bacc.Bacc("TRN2", target_bir_lowering=False, num_devices=1)
    arrays, args = {}, []
    for name in _INS:
        a = _np.ascontiguousarray(inputs[name]).reshape(_np.shape(inputs[name]) or (1,))
        arrays[f"in_{name}_dram"] = a
        args.append(nc.dram_tensor(f"in_{name}_dram", a.shape, _mybir.dt.from_np(a.dtype), kind="ExternalInput").ap())
    shape = tuple(inputs["x"].shape)
    args.append(nc.dram_tensor("out_0_dram", shape, _mybir.dt.float32, kind="ExternalOutput").ap())
    gnn_moe_kernel(nc, *args)
    r = _run(nc, [arrays], core_ids=[0])
    return r.results[0]["out_0_dram"]
```

```python
from contextlib import ExitStack

import concourse.bass as bass
from concourse import mybir

F32 = mybir.dt.float32
BF16 = mybir.dt.bfloat16
I32 = mybir.dt.int32
ALU = mybir.AluOpType
ACT = mybir.ActivationFunctionType
AX_X = mybir.AxisListType.X
ds = bass.ds

P = 128
LN_EPS = 1e-5
U = 9
R = 2 * U
GT = 5
G = 3
STEPS = 9
UB = 3


def gnn_moe_kernel(nc, x, src, dst, W1a, b1a, W1b, b1b, W2a, b2a, W2b, b2b, eps1, eps2,
                   Wg, bg, W1, b1, W2, b2, out):
    N, D = x.shape
    H = W1a.shape[1]
    E = Wg.shape[1]
    EDGES = src.shape[0]
    TILES = -(-N // P)
    FULL = N // P
    TAIL = N - FULL * P
    NP = TILES * P
    CHUNKS = -(-EDGES // P)
    EFULL = EDGES // P
    ETAIL = EDGES - EFULL * P
    ITEMS = CHUNKS + TILES
    TURNS = ITEMS // R
    GROUPS = TILES // GT
    GN = GT * P
    KD, KH = D // P, H // P
    BLK = 4
    EP = next(p for p in range(P, 0, -1) if EDGES % p == 0)
    EC = EDGES // EP
    BLOCKS = -(-(2 * N + E * (P - 1)) // (P * UB)) * UB
    RB = TILES + 1
    BTURNS = BLOCKS // UB
    BTURNS_MIN = -(-2 * N // (P * UB))
    RW = D + 2
    assert ITEMS == TURNS * R + U and TILES == GROUPS * GT and ITEMS + R <= BLK * P and U % G == 0
    assert H == 512 and D == 256 and E == 8 and ETAIL > 0 and TAIL > 0 and EFULL == CHUNKS - 1
    assert TURNS + 2 <= P

    with ExitStack() as ctx:
        def sb(name, shape, dt=F32):
            return ctx.enter_context(nc.sbuf_tensor(name, shape, dt))

        def S(name):
            return ctx.enter_context(nc.semaphore(name))

        xn_d = nc.dram_tensor("xn_d", [NP, D], F32).ap()
        g_d = nc.dram_tensor("g_d", [NP, H], F32).ap()
        edges_d = nc.dram_tensor("edges_d", [CHUNKS + 1, 2 * P], I32).ap()
        tables_d = nc.dram_tensor("tables_d", [(BLK + 2) * P], I32).ap()
        rows_d = nc.dram_tensor("rows_d", [(E * RB + 1) * P, RW], F32).ap()
        y_d = nc.dram_tensor("y_d", [2 * NP + BLOCKS * P, D], F32).ap()

        xs = sb("xs", [P, TILES, D])
        early = sb("early", [P, TILES * D + KD * H + KH * H])
        acc1 = early[:, 0:TILES * D].rearrange("p (t d) -> p t d", t=TILES)
        w1a = early[:, TILES * D:TILES * D + KD * H].rearrange("p (k n) -> p k n", k=KD)
        w1b = early[:, TILES * D + KD * H:TILES * D + (KD + KH) * H].rearrange("p (k n) -> p k n", k=KH)
        we1 = early[:, 0:E * KD * H].rearrange("p (e k n) -> p e k n", e=E, k=KD)
        late = sb("late", [P, TILES * H])
        acc2 = late[:, :].rearrange("p (t d) -> p t d", t=TILES)
        dst_i = late[0:EP, 0:EC].bitcast(I32)
        dst_tile = late[0:EP, EC:2 * EC].bitcast(BF16)[:, 0:EC]
        below = [late[0:EP, (t + 1) * EC:(t + 2) * EC].bitcast(BF16)[:, 0:EC] for t in range(TILES)]
        scratch = late[:, (TILES + 1) * EC:]
        item_cmp = scratch[:, 0:3 * BLK * TILES].rearrange("p (k b t) -> p k b t", k=3, b=BLK)
        per_tile = scratch[:, 3 * BLK * TILES:(3 * BLK + 6) * TILES].rearrange("p (k t) -> p k t", k=6)
        chunk_lo = scratch[:, (3 * BLK + 6) * TILES:(3 * BLK + 8) * TILES].rearrange("p (k t) -> p k t", k=2)
        rows = late[:, 0:TILES * RW].rearrange("p (t r) -> p t r", t=TILES)
        block_cmp = late[:, TILES * RW:TILES * RW + 2 * BLOCKS * E].rearrange("p (k b e) -> p k b e", k=2, b=BLOCKS)
        ys = late[:, :].rearrange("p (k t d) -> p k t d", k=2, t=TILES)
        ring = sb("ring", [P, U * H])
        flat = ring[:, :]
        slots = [[ring[:, s_ * D:s_ * D + D] for s_ in range(R)],
                 [(ring, early)[s_ // U][:, (s_ % U) * H:(s_ % U) * H + H] for s_ in range(R)]]
        item_edges_i = flat[:, 0:BLK * 2 * P].bitcast(I32).rearrange("p (b c) -> p b c", b=BLK)
        item_edges_f = flat[:, BLK * 2 * P:2 * BLK * 2 * P].rearrange("p (b c) -> p b c", b=BLK)
        gT = flat[:, 0:KD * GN].rearrange("p (k n) -> p k n", k=KD)
        xb = flat[:, 0:UB * RW].rearrange("p (u r) -> p u r", u=UB)
        yb = flat[:, UB * RW:UB * (RW + D)].rearrange("p (u d) -> p u d", u=UB)
        o = UB * (RW + D)
        xbT = flat[:, o:o + KD * P].rearrange("p (k n) -> p k n", k=KD)
        o += KD * P
        w_now = [flat[:, o + u * KD * H:o + (u + 1) * KD * H] for u in range(UB - 1)]
        assert o + (UB - 1) * KD * H <= U * H
        w2a_b2 = sb("w2a_b2", [P, KH * H])
        w2a = w2a_b2[:, :].rearrange("p (k n) -> p k n", k=KH)
        b2_all = w2a_b2[:, 0:E * D].rearrange("p (e d) -> p e d", e=E)
        w2b = sb("w2b", [P, KH, D])
        we2 = sb("we2", [P, E, KH, D])
        wg = sb("wg", [P, KD, E])
        b1a_c = sb("b1a_c", [P, KH])
        b2a_c = sb("b2a_c", [P, KH])
        b1_c = sb("b1_c", [P, E, KH])
        b1b_c = sb("b1b_c", [P, KH])
        b2b_all = sb("b2b_all", [P, D])
        bg_all = sb("bg_all", [P, E])
        scale1 = sb("scale1", [P, 1])
        scale2 = sb("scale2", [P, 1])
        ident = sb("ident", [P, P])
        ones = sb("ones", [P, P])
        before = sb("before", [P, P])
        node_id = sb("node_id", [P, P])
        item_id = sb("item_id", [P, BLK])
        turn_id = sb("turn_id", [P, 2])
        expert_id = sb("expert_id", [P, GT, E])
        row_of = sb("row_of", [P, 1])
        region = sb("region", [P, E])
        block_row = sb("block_row", [P, BLOCKS])
        pad_rows = sb("pad_rows", [2, 2 * P], I32)
        fill = sb("fill", [P, RW])
        cnt = sb("cnt", [P, TILES])
        bound = sb("bound", [P, TILES + 1])
        bound_i = sb("bound_i", [P, 2, TILES + 1], I32)
        item_sum = sb("item_sum", [P, 5, BLK])
        item_chunk_i = sb("item_chunk_i", [P, BLK], I32)
        tables_c = sb("tables_c", [P, BLK + 2], I32)
        tables = sb("tables", [1, (BLK + 2) * P], I32)
        idx = sb("idx", [P, R], I32)
        work = sb("work", [P, 2 * BLK * P + U * P])
        src_col = work[:, 0:BLK * P].bitcast(I32)
        dst_col = work[:, BLK * P:2 * BLK * P]
        onehot = work[:, 2 * BLK * P:].rearrange("p (u n) -> p u n", u=U)
        parts = [work[:, k * TILES * E:(k + 1) * TILES * E].rearrange("p (t e) -> p t e", e=E) for k in range(8)]
        gates, top, first, second, either, at, total = parts[0:7]
        top_i = work[:, 7 * TILES * E:8 * TILES * E].bitcast(mybir.dt.uint32).rearrange("p (t e) -> p t e", e=E)
        upto = work[:, 8 * TILES * E:(9 * TILES + 1) * E].rearrange("p (t e) -> p t e", e=E)
        o = (9 * TILES + 1) * E
        slot = work[:, o:o + 2 * TILES].rearrange("p (k t) -> p k t", k=2)
        slot_i = work[:, o + 2 * TILES:o + 4 * TILES].bitcast(I32).rearrange("p (k t) -> p k t", k=2)
        stats = sb("stats", [P, TILES, 6])
        mv = sb("mv", [P, TILES, 2])
        ln = sb("ln", [P, 5, TILES])
        stage = sb("stage", [P, H])
        aT = sb("aT", [P, KH, P])
        hT = sb("hT", [P, KH, P])
        hb = sb("hb", [P, 2, H])
        w_now.append(hb[:, :, :].rearrange("p j n -> p (j n)"))
        w_now = [w.rearrange("p (k n) -> p k n", k=KD) for w in w_now]
        hbT = [hT[:, :, :], aT[:, :, :], stage[:, :].rearrange("p (k n) -> p k n", k=KH)]
        per_expert = sb("per_expert", [P, 5, E])
        blocks_i = sb("blocks_i", [P, E], I32)
        ends_i = sb("ends_i", [P, E], I32)
        turns = sb("turns", [P, 2])
        turns_i = sb("turns_i", [P, 1], I32)
        real = sb("real", [P, 1])
        block_expert = sb("block_expert", [P, BLOCKS])
        block_pos = sb("block_pos", [P, 2, BLOCKS])
        block_pos_i = sb("block_pos_i", [P, BLOCKS], I32)
        block_expert_i = sb("block_expert_i", [P, BLOCKS], I32)
        dest = sb("dest", [P, 3, BLOCKS])
        dest_i = sb("dest_i", [P, UB], I32)

        bank = [ctx.enter_context(nc.psum_tensor(f"bank{i}", [P, 512], F32)) for i in range(8)]

        sum_bank = [[bank[b] for b in (0, 1, 2)], [bank[b] for b in (0, 1, 2, 3, 5, 7)]]
        assert all(R % len(banks) == 0 for banks in sum_bank) and STEPS == U

        NWEIGHTS = 13
        x_in, edges_in, pad_made, pad_put, dst_in, fill_put = (
            S("x_in"), S("edges_in"), S("pad_made"), S("pad_put"), S("dst_in"), S("fill_put"))
        consts, weights_in, prep, cnt_sum = S("consts"), S("weights_in"), S("prep"), S("cnt_sum")
        chunk_ids, items_in, items_T, tables_out, tables_in = (
            S("chunk_ids"), S("items_in"), S("items_T"), S("tables_out"), S("tables_in"))
        cols_made, tables_made = S("cols_made"), S("tables_made")
        stats_made, var_made, root_made, xn_made, xn_put = (
            S("stats_made"), S("var_made"), S("root_made"), S("xn_made"), S("xn_put"))
        scaled = S("scaled")
        gathered = [[S(f"gathered{L}_{u}") for u in range(R)] for L in range(2)]
        idx_ready = [S(f"idx_ready{L}") for L in range(2)]
        item_ready = [S(f"item_ready{L}") for L in range(2)]
        item_summed = [S(f"item_summed{L}") for L in range(2)]
        item_added = [S(f"item_added{L}") for L in range(2)]
        staged = [S(f"staged{L}") for L in range(2)]
        turned = [S(f"turned{L}") for L in range(2)]
        turned_out, up, mid, mid_out, residual_ready = (
            S("turned_out"), S("up"), S("mid"), S("mid_out"), S("residual_ready"))
        up_out = [S(f"up_out{L}") for L in range(2)]
        down = [S(f"down{L}") for L in range(2)]
        down_free = [S(f"down_free{L}") for L in range(2)]
        g_scaled = S("g_scaled")
        g_put = [S(f"g_put{j}") for j in range(2)]
        x2_var, x2_root, xn2_made, xn2_turned, xn2_out, gate_sum, gate_out, rows_made = (
            S("x2_var"), S("x2_root"), S("xn2_made"), S("xn2_turned"), S("xn2_out"), S("gate_sum"), S("gate_out"),
            S("rows_made"))
        picked, placed, slots_made, ends_made, blocks_made, scattered = (
            S("picked"), S("placed"), S("slots_made"), S("ends_made"), S("blocks_made"), S("scattered"))
        expert1_in, expert2_in, bias2_in = S("expert1_in"), S("expert2_in"), S("bias2_in")
        block_in = [S(f"block_in{u}") for u in range(UB)]
        bx_turned, bx_out, w_copied, bh, bg_out, by, by_out, dest_made = (
            S("bx_turned"), S("bx_out"), S("w_copied"), S("bh"), S("bg_out"), S("by"), S("by_out"), S("dest_made"))
        block_put = [S(f"block_put{u}") for u in range(UB)]
        ys_in = [S(f"ys_in{g}") for g in range(len(range(0, FULL, GT)) + 1)]
        first_added, summed, out_put = S("first_added"), S("summed"), S("out_put")
        dve = S("dve")

        def tile(a, t, n=1):
            return a[:, ds(t, n), :].rearrange("p t d -> p (t d)")

        parts_out = [(t0, min(t0 + GT, FULL), P) for t0 in range(0, FULL, GT)] + [(FULL, TILES, TAIL)]

        def middle_turns(engine):
            engine.wait_ge(blocks_made, 1)
            return engine.value_load(turns_i[0:1, 0:1], min_val=BTURNS_MIN - 2, max_val=BTURNS - 2)

        block = ctx.enter_context(nc.Block())

        @block.sync
        def _(sp):
            sp.dma_start(dst_i, dst.rearrange("(p c) -> p c", p=EP)).then_inc(dst_in, 16)
            sp.dma_start(xs[:, 0:FULL, :], x[0:FULL * P, :].rearrange("(t p) d -> p t d", p=P)).then_inc(x_in, 16)
            sp.wait_ge(pad_made, 3)
            sp.dma_start(xs[0:TAIL, FULL, :], x[FULL * P:N, :]).then_inc(x_in, 16)
            sp.dma_start(edges_d[CHUNKS - 1:CHUNKS + 1, :], pad_rows[:, :]).then_inc(pad_put, 16)
            for c, a in enumerate((src, dst)):
                sp.dma_start(edges_d[0:EFULL, c * P:c * P + P],
                             a[0:EFULL * P].rearrange("(c e) -> c e", e=P)).then_inc(edges_in, 16)
            sp.wait_ge(pad_put, 16)
            for c, a in enumerate((src, dst)):
                sp.dma_start(edges_d[EFULL:EFULL + 1, c * P:c * P + ETAIL],
                             a[EFULL * P:EDGES].rearrange("(c e) -> c e", c=1)).then_inc(edges_in, 16)
            with nc.allow_non_contiguous_dma(reason="biases as columns, one scalar for all partitions"):
                loads = [
                    (scale1[:, :], eps1.rearrange("(a b) -> a b", a=1).to_broadcast([P, 1])),
                    (scale2[:, :], eps2.rearrange("(a b) -> a b", a=1).to_broadcast([P, 1])),
                    (w1a, W1a.rearrange("(k p) n -> p k n", p=P)),
                    (w1b, W1b.rearrange("(k p) n -> p k n", p=P)),
                    (w2a, W2a.rearrange("(k p) n -> p k n", p=P)),
                    (w2b[:, :, :], W2b.rearrange("(k p) n -> p k n", p=P)),
                    (wg[:, :, :], Wg.rearrange("(k p) n -> p k n", p=P)),
                    (b1a_c[:, :], b1a.rearrange("(k p) -> p k", p=P)),
                    (b2a_c[:, :], b2a.rearrange("(k p) -> p k", p=P)),
                    (b1_c[:, :, :], b1.rearrange("e (k p) -> p e k", p=P)),
                    (b1b_c[:, :], b1b.rearrange("(k p) -> p k", p=P)),
                    (b2b_all[:, :], b2b.rearrange("(a n) -> a n", a=1).to_broadcast([P, D])),
                    (bg_all[:, :], bg.rearrange("(a n) -> a n", a=1).to_broadcast([P, E])),
                ]
                assert len(loads) == NWEIGHTS
                for to, of in loads:
                    sp.dma_start(to, of).then_inc(weights_in, 16)
                sp.wait_ge(tables_made, 1)
                sp.dma_start(tables_d.rearrange("(b p) -> p b", p=P), tables_c[:, :]).then_inc(tables_out, 16)
                sp.wait_ge(tables_out, 16)
                sp.dma_start(tables[:, :], tables_d.rearrange("(a n) -> a n", a=1)).then_inc(tables_in, 16)
            for g in range(GROUPS):
                sp.wait_ge(xn_made, g + 1)
                sp.dma_start(xn_d[g * GN:g * GN + GN, :].rearrange("(t p) d -> p t d", p=P),
                             acc1[:, g * GT:g * GT + GT, :]).then_inc(xn_put, 16)
            sp.wait_ge(consts, 14)
            sp.dma_start(rows_d[E * RB * P:(E * RB + 1) * P, :], fill[:, :]).then_inc(fill_put, 16)
            gd = g_d.rearrange("(t p) d -> t p d", p=P)

            def put_tile(t, j):
                sp.wait_ge(down_free[0], t + 2)
                sp.dma_start(gd[ds(t, 1), :, :].rearrange("t p d -> (t p) d"), hb[:, j, :]).then_inc(g_put[j], 16)

            assert TILES == 3 * E + 1
            with sp.Fori(0, E // 2) as n:
                for q in range(6):
                    put_tile(n * 6 + q, q % 2)
                    if q % 3 == 2:
                        sp.dma_start(we2[:, ds(n * 2 + q // 3, 1), :, :].rearrange("p e k n -> p (e k) n"),
                                     W2[ds(n * 2 + q // 3, 1), :, :].rearrange("e (k p) n -> p (e k) n", p=P)).then_inc(expert2_in, 16)
            put_tile(TILES - 1, 0)
            sp.wait_ge(item_summed[1], ITEMS)
            sp.dma_start(we1.rearrange("p e k n -> p (e k) n"),
                         W1.rearrange("e (k p) n -> p (e k) n", p=P)).then_inc(expert1_in, 16)
            sp.wait_ge(down[1], TILES)
            sp.dma_start(w2a_b2[:, 0:E * D], b2.rearrange("e d -> (e d)").rearrange("(a n) -> a n", a=1)
                         .to_broadcast([P, E * D])).then_inc(bias2_in, 16)

            def load_block(m, c):
                u = c % UB
                pos = sp.value_load(block_pos_i[0:1, ds(m * UB + c, 1)], min_val=0, max_val=E * RB)
                if c >= UB:
                    sp.wait_ge(bx_turned, m * UB + (c + 1 - UB))
                    sp.wait_ge(dest_made, m * UB + (c + 1 - UB))
                sp.dma_start(xb[:, u, :], rows_d.rearrange("(b p) r -> b p r", p=P)[ds(pos, 1), :, :]
                             .rearrange("b p r -> (b p) r")).then_inc(block_in[u], 16)

            sp.wait_ge(ends_made, 1)
            for e in range(E):
                end = sp.value_load(ends_i[0:1, e:e + 1], min_val=e * RB * P, max_val=e * RB * P + N)
                sp.dma_start(rows_d[ds(end, P), :], fill[:, :]).then_inc(fill_put, 16)
            middle = middle_turns(sp)
            sp.wait_ge(scattered, 16 * 2 * TILES)
            sp.wait_ge(fill_put, 16 * (E + 1))
            for u in range(UB):
                load_block(0, u)
            with sp.Fori(0, middle + 1) as m:
                for u in range(UB):
                    load_block(m, UB + u)
            for u in range(UB):
                sp.wait_ge(block_put[u], middle * 16 + 32)
            for g, (t0, t1, n) in enumerate(parts_out):
                for k in range(2):
                    r0 = k * NP + t0 * P
                    sp.dma_start(ys[0:n, k, t0:t1, :],
                                 y_d[r0:r0 + (t1 - t0 - 1) * P + n, :].rearrange("(t p) d -> p t d", p=n)).then_inc(ys_in[g], 16)
            for g, (t0, t1, n) in enumerate(parts_out):
                sp.wait_ge(summed, g + 1)
                sp.dma_start(out[t0 * P:(t1 - 1) * P + n, :].rearrange("(t p) d -> p t d", p=n),
                             xs[0:n, t0:t1, :]).then_inc(out_put, 16)
            sp.wait_ge(out_put, 16 * len(parts_out))

        @block.gpsimd
        def _(pool):
            pool.memset(pad_rows[:, 0:P], 0).then_inc(pad_made, 1)
            pool.memset(pad_rows[:, P:2 * P], -1).then_inc(pad_made, 1)
            pool.memset(xs[:, FULL, :], 0.0).then_inc(pad_made, 1)
            pool.memset(ones[:, :], 1.0).then_inc(consts, 1)
            pool.memset(ident[:, :], 0.0).then_inc(consts, 1)
            f32 = dict(allow_small_or_imprecise_dtypes=True)
            pool.iota(node_id[:, :], [[1, P]], base=0, channel_multiplier=0, **f32).then_inc(consts, 1)
            pool.iota(item_id[:, :], [[P, BLK]], base=0, channel_multiplier=1, **f32).then_inc(consts, 1)
            pool.iota(turn_id[:, 0:1], [[1, 1]], base=0, channel_multiplier=R, **f32).then_inc(consts, 1)
            pool.iota(expert_id[:, :, :], [[0, GT], [1, E]], base=0, channel_multiplier=0, **f32).then_inc(consts, 1)
            pool.iota(block_row[:, :], [[P, BLOCKS]], base=0, channel_multiplier=0, **f32).then_inc(consts, 1)
            pool.iota(row_of[:, :], [[1, 1]], base=0, channel_multiplier=1, **f32).then_inc(consts, 1)
            pool.iota(region[:, :], [[RB * P, E]], base=0, channel_multiplier=0, **f32).then_inc(consts, 1)
            pool.memset(fill[:, 0:D], 0.0).then_inc(consts, 1)
            pool.iota(fill[:, D:D + 1], [[1, 1]], base=NP, channel_multiplier=1, **f32).then_inc(consts, 1)
            pool.memset(fill[:, D + 1:D + 2], -1.0).then_inc(consts, 1)
            pool.memset(stats[:, :, :], 0.0).then_inc(down_free[0], 1)
            pool.memset(mv[:, :, :], 0.0).then_inc(down_free[1], 1)
            pool.wait_ge(consts, 12)
            pool.affine_select(out=ident[:, :], in_=ident[:, :], compare_op=ALU.not_equal, fill=1.0,
                               base=0, pattern=[[-1, P]], channel_multiplier=1).then_inc(consts, 1)
            pool.affine_select(out=before[:, :], in_=ones[:, :], compare_op=ALU.is_gt, fill=0.0,
                               base=0, pattern=[[1, P]], channel_multiplier=-1).then_inc(consts, 1)
            pool.wait_ge(edges_in, 64)
            pool.wait_ge(pad_put, 16)
            pool.wait_ge(chunk_ids, 1)
            for b in range(BLK):
                pool.indirect_dma_start(item_edges_i[:, b, :], None, edges_d[:, :],
                                        bass.IndirectOffsetOnAxis(item_chunk_i[:, b:b + 1], 0)).then_inc(items_in, 16)

            def gathers(L):
                table = (xn_d, g_d)[L]

                def gather(n, s_):
                    if s_ % G == 0:
                        pool.wait_ge(idx_ready[L], n * (R // G) + (s_ // G + 1))
                        pool.nop(nofuse=True)
                    pool.indirect_dma_start(slots[L][s_], None, table[:, :],
                                            bass.IndirectOffsetOnAxis(idx[:, s_:s_ + 1], 0)).then_inc(gathered[L][s_], 16)

                with pool.Fori(0, TURNS) as n:
                    for s_ in range(R):
                        gather(n, s_)
                for s_ in range(U):
                    gather(TURNS, s_)

            pool.wait_ge(xn_put, 16 * GROUPS)
            gathers(0)
            for j in range(2):
                pool.wait_ge(g_put[j], 16 * ((TILES + 1 - j) // 2))
            gathers(1)
            pool.wait_ge(staged[1], TILES)
            pool.iota(rows[:, :, D:D + 1], [[P, TILES], [0, 1]], base=0, channel_multiplier=1, **f32).then_inc(rows_made, 1)
            pool.wait_ge(rows_made, 1)
            for g in range(GROUPS):
                pool.wait_ge(slots_made, g + 1)
                for t in range(g * GT, g * GT + GT):
                    n = P if t < FULL else TAIL
                    for k in range(2):
                        pool.indirect_dma_start(rows_d[:, :], bass.IndirectOffsetOnAxis(slot_i[0:n, k, t:t + 1], 0),
                                                rows[0:n, t, :], None).then_inc(scattered, 16)
            middle = middle_turns(pool)
            with pool.Fori(0, middle + 2) as n:
                for u in range(UB):
                    pool.wait_ge(by_out, n * UB + (u + 1))
                    pool.nop(nofuse=True)
                    pool.indirect_dma_start(y_d[:, :], bass.IndirectOffsetOnAxis(dest_i[:, u:u + 1], 0),
                                            yb[:, u, :], None).then_inc(block_put[u], 16)

        @block.scalar
        def _(act):
            act.wait_ge(var_made, 1)
            act.activation(ln[:, 1, :], ln[:, 0, :], ACT.Sqrt).then_inc(root_made, 1)
            act.wait_ge(weights_in, 16 * NWEIGHTS)
            act.wait_ge(scaled, 2)
            act.wait_ge(tables_in, 16)

            def stage_tile(L, t, first):
                acc, W = ((acc1, D), (acc2, H))[L]
                end = act.value_load(tables[0:1, ds(t + (BLK + 1) * P, 1)], min_val=1, max_val=ITEMS)
                act.wait_ge(item_added[L], end)
                if not first:
                    act.wait_ge(turned[L], t)
                act.copy(stage[:, 0:W], tile(acc, t)).then_inc(staged[L], 1)

            def relus(t, half, sem, out, of, bias, done):
                act.wait_ge(sem, t * 2 + (half + 1))
                for m in (2 * half, 2 * half + 1):
                    act.activation(out[:, m, :], bank[of][:, (m % 2) * P:(m % 2) * P + P], ACT.Relu,
                                   bias=bias[:, m:m + 1]).then_inc(done, 1)

            def hidden(t, j, first):
                act.wait_ge(turned[0], t + 1)
                act.copy(aT[:, 0:KD, :], bank[4][:, 0:KD * P].rearrange("p (k n) -> p k n", k=KD)).then_inc(turned_out, 1)
                for half in range(2):
                    relus(t, half, up, hT, 4 + half, b1a_c, up_out[0])
                for half in range(2):
                    relus(t, half, mid, aT, (3, 7)[half], b1b_c, mid_out)
                act.wait_ge(down[0], t + 1)
                if not first:
                    act.wait_ge(g_put[j], (t - j) * 8)
                    act.wait_ge(g_scaled, t - 1)
                act.copy(hb[:, j, :], bank[6][:, :]).then_inc(down_free[0], 1)
                act.wait_ge(down_free[0], t + 2)
                act.activation(tile(acc2, t), hb[:, j, :], ACT.Copy, scale=scale2[:, :]).then_inc(g_scaled, 1)

            stage_tile(0, 0, True)
            hidden(0, 0, True)
            stage_tile(0, 1, False)
            hidden(1, 1, True)
            with act.Fori(2, TILES - 1, 2) as t:
                for j in range(2):
                    stage_tile(0, t + j, False)
                    hidden(t + j, j, False)
            stage_tile(0, TILES - 1, False)
            hidden(TILES - 1, 0, False)

            def residual(t):
                act.wait_ge(turned[1], t + 1)
                for m in range(KH):
                    act.activation(hT[:, m, :], bank[4][:, m * P:m * P + P], ACT.Relu,
                                   bias=b2a_c[:, m:m + 1]).then_inc(up_out[1], 1)
                act.wait_ge(down[1], t + 1)
                act.copy(tile(xs, t), bank[6][:, 0:D]).then_inc(down_free[1], 1)

            stage_tile(1, 0, True)
            residual(0)
            with act.Fori(1, TILES) as t:
                stage_tile(1, t, False)
                residual(t)
            act.wait_ge(x2_var, 1)
            act.activation(ln[:, 1, :], ln[:, 0, :], ACT.Sqrt).then_inc(x2_root, 1)
            for g in range(GROUPS):
                if g:
                    act.wait_ge(gate_sum, g)
                for j in range(GT):
                    act.wait_ge(xn2_turned, g * GT + (j + 1))
                    act.copy(gT[:, :, j * P:j * P + P],
                             bank[3 + (g * GT + j) % 2][:, 0:KD * P].rearrange("p (k n) -> p k n", k=KD)).then_inc(xn2_out, 1)

            def take_x(m, c):
                act.wait_ge(bx_turned, m * UB + (c + 1))
                act.copy(xbT, bank[3][:, 0:KD * P].rearrange("p (k n) -> p k n", k=KD)).then_inc(bx_out, 1)

            def gelu(m, c):
                u = c % UB
                e = act.value_load(block_expert_i[0:1, ds(m * UB + c, 1)], min_val=0, max_val=E - 1)
                act.wait_ge(bh, m * UB + (c + 1))
                if c >= UB:
                    act.wait_ge(by, m * UB + (c + 1 - UB))
                act.nop(nofuse=True)
                for k in range(KH):
                    act.activation(hbT[u][:, k, :], bank[u][:, k * P:k * P + P], ACT.Gelu,
                                   bias=b1_c[:, ds(e, 1), k:k + 1].rearrange("p e k -> p (e k)")).then_inc(bg_out, 1)

            middle = middle_turns(act)
            take_x(0, 0)
            take_x(0, 1)
            gelu(0, 0)
            for c in range(UB):
                take_x(0, c + 2)
                gelu(0, c + 1)
            with act.Fori(0, middle) as m:
                for c in range(UB, 2 * UB):
                    take_x(m, c + 2)
                    gelu(m, c + 1)
            take_x(middle, 2 * UB - 1)
            gelu(middle, 2 * UB - 2)
            gelu(middle, 2 * UB - 1)

        @block.tensor
        def _(pe):
            pe.wait_ge(consts, 14)
            pe.wait_ge(prep, 1)
            pe.matmul(bank[0][:, 0:TILES - 1], ones[0:EP, :], cnt[0:EP, 0:TILES - 1], start=True, stop=True).then_inc(cnt_sum, 1)
            pe.wait_ge(prep, 2)
            for b in range(BLK):
                for c in range(2):
                    pe.transpose(bank[1 + c][:, b * P:b * P + P], item_edges_f[:, b, c * P:c * P + P],
                                 ident[:, :]).then_inc(items_T, 1)

            def sum_item(L, n, s_, first):
                W = (D, H)[L]
                if s_ % G == 0:
                    pe.wait_ge(item_ready[L], n * (R // G) + (s_ // G + 1))
                banks = sum_bank[L]
                if not (first and s_ < len(banks)):
                    pe.wait_ge(item_added[L], n * R + (s_ + 1 - len(banks)))
                pe.wait_ge(gathered[L][s_], n * 16 + 16)
                pe.matmul(banks[s_ % len(banks)][:, 0:W], onehot[:, s_ % U, :], slots[L][s_],
                          start=True, stop=True).then_inc(item_summed[L], 1)

            def turn_tile(L, t):
                pe.wait_ge(staged[L], t + 1)
                for k in range((KD, KH)[L]):
                    mm = pe.transpose(bank[4][:, k * P:k * P + P], stage[:, k * P:k * P + P], ident[:, :])
                mm.then_inc(turned[L], 1)

            def up_product(t, half):
                if half == 0:
                    pe.wait_ge(turned_out, t + 1)
                for m in (2 * half, 2 * half + 1):
                    for k in range(KD):
                        mm = pe.matmul(bank[4 + half][:, (m % 2) * P:(m % 2) * P + P], w1a[:, k, m * P:m * P + P],
                                       aT[:, k, :], start=(k == 0), stop=(k == KD - 1))
                mm.then_inc(up, 1)

            def mid_product(t, half):
                if half == 0:
                    pe.wait_ge(up_out[0], t * KH + KH)
                for m in (2 * half, 2 * half + 1):
                    for k in range(KH):
                        mm = pe.matmul(bank[(3, 7)[half]][:, (m % 2) * P:(m % 2) * P + P], w1b[:, k, m * P:m * P + P],
                                       hT[:, k, :], start=(k == 0), stop=(k == KH - 1))
                mm.then_inc(mid, 1)

            def down_product(L, t, ks):
                of, wd, done, W = ((aT, w2a, mid_out, H), (hT, w2b, up_out[1], D))[L]
                if ks[0] == 0:
                    pe.wait_ge(down_free[L], t + 1)
                    if L == 1:
                        pe.matmul(bank[6][:, 0:W], ident[:, :], tile(xs, t), start=True, stop=False)
                for k in ks:
                    pe.wait_ge(done, t * KH + (k + 1))
                    mm = pe.matmul(bank[6][:, 0:W], of[:, k, :], wd[:, k, :], start=(L == 0 and k == 0), stop=(k == KH - 1))
                if k == KH - 1:
                    mm.then_inc(down[L], 1)

            def dense_step(L, t, step):
                if step == 0:
                    turn_tile(L, t)
                elif L == 0:
                    if step in (1, 2):
                        up_product(t, step - 1)
                    elif step in (4, 5):
                        mid_product(t, step - 4)
                    elif step in (7, 8):
                        down_product(L, t, (2 * (step - 7), 2 * (step - 7) + 1))
                elif step >= STEPS - KH:
                    down_product(L, t, (step - STEPS + KH,))

            def dense(L, t):
                for step in range(STEPS):
                    dense_step(L, t, step)

            def complete_tiles(L, lo, hi):
                with pe.If(lo < hi):
                    with pe.Fori(lo, hi) as t:
                        dense(L, t)

            def turn(L, n, items):
                lo = pe.value_load(tables[0:1, ds(n + (BLK * P - 1), 1)], min_val=0, max_val=TILES - 1)
                hi = pe.value_load(tables[0:1, ds(n + BLK * P, 1)], min_val=0, max_val=TILES - 1)
                with pe.If(lo < hi):
                    if items == R:
                        with pe.If(lo + 1 < hi):
                            first = pe.value_load(tables[0:1, ds(n + (BLK * P - 1), 1)], min_val=0, max_val=TILES - 2)
                            for s_ in range(R):
                                sum_item(L, n, s_, False)
                                dense_step(L, first + s_ // STEPS, s_ % STEPS)
                            complete_tiles(L, lo + 2, hi)
                        with pe.Else():
                            for s_ in range(R):
                                sum_item(L, n, s_, False)
                                if s_ % 2 == 0:
                                    dense_step(L, lo, s_ // 2)
                    else:
                        for s_ in range(items):
                            sum_item(L, n, s_, False)
                            dense_step(L, lo, s_)
                        complete_tiles(L, lo + 1, hi)
                with pe.Else():
                    for s_ in range(items):
                        sum_item(L, n, s_, False)

            pe.wait_ge(weights_in, 16 * NWEIGHTS)
            pe.wait_ge(tables_in, 16)
            for L in range(2):
                if L == 1:
                    pe.wait_ge(residual_ready, 1)
                for s_ in range(R):
                    sum_item(L, 0, s_, True)
                with pe.Fori(1, TURNS) as n:
                    turn(L, n, R)
                turn(L, TURNS, U)
                done = pe.value_load(tables[0:1, BLK * P + TURNS:BLK * P + TURNS + 1], min_val=0, max_val=TILES - 1)
                with pe.Fori(done, TILES) as t:
                    dense(L, t)

            def turn_group(g):
                pe.wait_ge(xn2_made, g + 1)
                for t in range(g * GT, g * GT + GT):
                    if t >= 2:
                        pe.wait_ge(xn2_out, t - 1)
                    for k in range(KD):
                        mm = pe.transpose(bank[3 + t % 2][:, k * P:k * P + P], rows[:, t, k * P:k * P + P], ident[:, :])
                    mm.then_inc(xn2_turned, 1)

            def gate_group(g):
                if g:
                    pe.wait_ge(gate_out, g)
                for j in range(GT):
                    pe.wait_ge(xn2_out, g * GT + (j + 1))
                    for k in range(KD):
                        mm = pe.matmul(bank[6][:, j * E:j * E + E], gT[:, k, j * P:j * P + P], wg[:, k, :],
                                       start=(k == 0), stop=(k == KD - 1))
                mm.then_inc(gate_sum, 1)

            def place_group(g):
                pe.wait_ge(picked, g + 1)
                chosen = either[:, g * GT:g * GT + GT, :].rearrange("p t e -> p (t e)")
                pe.matmul(bank[0][:, 0:GT * E], before[:, :], chosen, start=True, stop=True).then_inc(placed, 1)
                pe.matmul(bank[1][:, 0:GT * E], ones[:, :], chosen, start=True, stop=True).then_inc(placed, 1)

            turn_group(0)
            gate_group(0)
            for g in range(GROUPS):
                if g + 1 < GROUPS:
                    turn_group(g + 1)
                place_group(g)
                if g + 1 < GROUPS:
                    gate_group(g + 1)

            def turn_x(m, c):
                u = c % UB
                pe.wait_ge(block_in[u], m * 16 + (c // UB + 1) * 16)
                for k in range(KD):
                    mm = pe.transpose(bank[3][:, k * P:k * P + P], xb[:, u, k * P:k * P + P], ident[:, :])
                mm.then_inc(bx_turned, 1)

            def first_product(m, c):
                u = c % UB
                pe.wait_ge(bx_out, m * UB + (c + 1))
                pe.wait_ge(w_copied, m * UB + (c + 1))
                if c >= UB:
                    pe.wait_ge(bg_out, m * (UB * KH) + (c + 1 - UB) * KH)
                for q in range(KH):
                    for k in range(KD):
                        mm = pe.matmul(bank[u][:, q * P:q * P + P], w_now[u][:, k, q * P:q * P + P], xbT[:, k, :],
                                       start=(k == 0), stop=(k == KD - 1))
                mm.then_inc(bh, 1)

            def second_product(m, c):
                u = c % UB
                e = pe.value_load(block_expert_i[0:1, ds(m * UB + c, 1)], min_val=0, max_val=E - 1)
                if c >= UB:
                    pe.wait_ge(by_out, m * UB + (c + 1 - UB))
                for k in range(KH):
                    pe.wait_ge(bg_out, m * (UB * KH) + (c * KH + k + 1))
                    mm = pe.matmul(bank[5 + u][:, 0:D], hbT[u][:, k, :], we2[:, ds(e, 1), k, :].rearrange("p e n -> p (e n)"),
                                   start=(k == 0), stop=(k == KH - 1))
                mm.then_inc(by, 1)

            def step(m, c):
                first_product(m, c + 1)
                turn_x(m, c + 2)
                second_product(m, c)

            middle = middle_turns(pe)
            pe.wait_ge(expert2_in, 16 * E)
            turn_x(0, 0)
            first_product(0, 0)
            turn_x(0, 1)
            for c in range(UB):
                step(0, c)
            with pe.Fori(0, middle) as m:
                for c in range(UB, 2 * UB):
                    step(m, c)
            step(middle, UB)
            first_product(middle, 2 * UB - 1)
            second_product(middle, 2 * UB - 2)
            second_product(middle, 2 * UB - 1)

        @block.vector
        def _(v):
            made = [0]

            def then(ins):
                made[0] += 1
                ins.then_inc(dve, 1)
                v.wait_ge(dve, made[0])

            v.wait_ge(dst_in, 16)
            then(v.tensor_scalar(dst_i, dst_i, 7, None, ALU.arith_shift_right))
            then(v.tensor_copy(dst_tile, dst_i))
            for t in range(1, TILES):
                ins = v.tensor_scalar(below[t], dst_tile, float(t), None, ALU.is_lt, ALU.add, accum_out=cnt[0:EP, t - 1:t])
            ins.then_inc(prep, 1)
            v.memset(bound[:, 0:1], 0.0)
            v.memset(bound[:, TILES:TILES + 1], float(EDGES))
            v.wait_ge(consts, 14)
            v.tensor_scalar(turn_id[:, 1:2], turn_id[:, 0:1], 0.0, -1.0, ALU.is_equal, ALU.mult)
            v.wait_ge(cnt_sum, 1)
            then(v.tensor_copy(bound[:, 1:TILES], bank[0][:, 0:TILES - 1]))
            v.tensor_copy(bound_i[:, 0, :], bound[:, :])
            v.tensor_tensor(turn_id[:, 0:1], turn_id[:, 0:1], turn_id[:, 1:2], ALU.add)
            then(v.tensor_scalar(bound_i[:, 1, :], bound[:, :], float(P - 1), None, ALU.add))
            then(v.tensor_scalar(bound_i[:, :, :], bound_i[:, :, :], 7, None, ALU.arith_shift_right))
            v.tensor_copy(chunk_lo[:, 0, :], bound_i[:, 0, 0:TILES])
            then(v.tensor_copy(chunk_lo[:, 1, :], bound_i[:, 1, 1:TILES + 1]))
            n_, end_, start_, off_, step_, wait_ = (per_tile[:, k, :] for k in range(6))
            then(v.tensor_tensor(n_, chunk_lo[:, 1, :], chunk_lo[:, 0, :], ALU.subtract))
            then(v.tensor_tensor_scan(end_, n_, n_, 0.0, ALU.add, ALU.bypass))
            v.tensor_scalar(wait_[:, 0:TILES - 1], end_[:, 0:TILES - 1], 1.0, None, ALU.max)
            v.memset(wait_[:, TILES - 1:TILES], float(ITEMS))
            then(v.tensor_tensor(start_, end_, n_, ALU.subtract))
            then(v.tensor_tensor(off_, chunk_lo[:, 0, :], start_, ALU.subtract))
            then(v.tensor_tensor(step_[:, 1:TILES], off_[:, 1:TILES], off_[:, 0:TILES - 1], ALU.subtract))
            for b in range(BLK):
                v.tensor_scalar(item_cmp[:, 0, b, 1:TILES], start_[:, 1:TILES], item_id[:, b:b + 1], None, ALU.is_le)
                ins = v.scalar_tensor_tensor(out=item_cmp[:, 1, b, 1:TILES], in0=start_[:, 1:TILES], scalar=item_id[:, b:b + 1],
                                             in1=step_[:, 1:TILES], op0=ALU.is_le, op1=ALU.mult)
            v.tensor_scalar(item_cmp[:, 2, 0, :], wait_, turn_id[:, 0:1], None, ALU.is_le)
            then(v.tensor_tensor(item_cmp[:, 2, 1, :], wait_, ident[:, 0:TILES], ALU.mult))
            tile_, jump_, past_, chunk_, first_node = (item_sum[:, k, :] for k in range(5))
            v.tensor_reduce(tile_, item_cmp[:, 0, :, 1:TILES], AX_X, ALU.add)
            v.tensor_reduce(jump_, item_cmp[:, 1, :, 1:TILES], AX_X, ALU.add)
            v.tensor_reduce(bound[:, 0:2], item_cmp[:, 2, 0:2, :], AX_X, ALU.add)
            then(v.tensor_scalar(past_, item_id[:, :], end_[:, TILES - 1:TILES], float(2 * CHUNKS), ALU.is_ge, ALU.mult))
            v.tensor_copy(tables_c[:, BLK:BLK + 2], bound[:, 0:2])
            v.tensor_copy(tables_c[:, 0:BLK], tile_).then_inc(tables_made, 1)
            then(v.tensor_tensor(chunk_, item_id[:, :], jump_, ALU.add))
            then(v.tensor_tensor(chunk_, chunk_, past_, ALU.add))
            v.tensor_scalar(item_chunk_i[:, :], chunk_, float(CHUNKS), None, ALU.min).then_inc(chunk_ids, 1)
            then(v.tensor_scalar(first_node, tile_, float(P), None, ALU.mult))

            def statistics(made_sem, sources, base, ready=None):
                with v.Fori(0, GROUPS) as g:
                    if ready:
                        v.wait_ge(ready, g * GT + (GT + 1))
                    for j in range(GT):
                        v.bn_stats(tile(stats, g * GT + j), tile(sources, g * GT + j)).then_inc(made_sem, 1)
                v.wait_ge(made_sem, base + TILES)

            def rstd_of(roots, made_sem):
                veps, root, rec, quo, rstd = (ln[:, k, :] for k in range(5))
                mean, half_gap = mv[:, :, 0], mv[:, :, 1]
                st = [stats[:, :, k] for k in range(6)]
                v.tensor_tensor(mean, st[1], st[4], ALU.add)
                v.tensor_tensor(half_gap, st[1], st[4], ALU.subtract)
                then(v.tensor_tensor(veps, st[2], st[5], ALU.add))
                v.tensor_scalar(mean, mean, 0.5, None, ALU.mult)
                then(v.tensor_scalar(half_gap, half_gap, 0.5, None, ALU.mult))
                v.tensor_scalar(veps, veps, 1.0 / D, LN_EPS, ALU.mult, ALU.add)
                then(v.tensor_tensor(half_gap, half_gap, half_gap, ALU.mult))
                v.tensor_tensor(veps, veps, half_gap, ALU.add).then_inc(made_sem, 1)
                v.wait_ge(roots, 1)
                then(v.reciprocal(rec, root))
                then(v.tensor_tensor(quo, veps, rec, ALU.mult))
                then(v.tensor_tensor(quo, quo, root, ALU.add))
                then(v.tensor_scalar(quo, quo, 0.5, None, ALU.mult))
                then(v.reciprocal(rstd, quo))

            v.wait_ge(x_in, 32)
            v.wait_ge(down_free[0], 1)
            v.wait_ge(down_free[1], 1)
            statistics(stats_made, xs, 0)
            rstd_of(root_made, var_made)
            with v.Fori(0, GROUPS) as g:
                for j in range(GT):
                    t = g * GT + j
                    ins = v.tensor_scalar(tile(acc1, t), tile(xs, t), mv[:, ds(t, 1), 0:1].rearrange("p t d -> p (t d)"),
                                          ln[:, 4, ds(t, 1)], ALU.subtract, ALU.mult)
                ins.then_inc(xn_made, 1)
            v.wait_ge(items_in, 16 * BLK)
            v.tensor_copy(item_edges_f[:, :, 0:P], item_edges_i[:, :, 0:P])
            for b in range(BLK):
                ins = v.tensor_scalar(item_edges_f[:, b, P:2 * P], item_edges_i[:, b, P:2 * P], first_node[:, b:b + 1], None,
                                      ALU.subtract)
            ins.then_inc(prep, 1)
            v.wait_ge(items_T, 2 * BLK)
            v.tensor_copy(src_col, bank[1][:, :]).then_inc(cols_made, 1)
            v.tensor_copy(dst_col, bank[2][:, :]).then_inc(cols_made, 1)
            v.wait_ge(weights_in, 16 * NWEIGHTS)

            def sources(L, i, s_):
                v.tensor_copy(idx[:, s_:s_ + G], src_col[:, ds(i, G)]).then_inc(idx_ready[L], 1)

            def target(L, i, u):
                ins = v.tensor_scalar(onehot[:, u, :], node_id[:, :], dst_col[:, ds(i, 1)], None, ALU.is_equal)
                if u % G == G - 1:
                    ins.then_inc(item_ready[L], 1)

            def first_items(L):
                for s_ in range(0, R, G):
                    sources(L, s_, s_)
                for u in range(U):
                    target(L, u, u)

            tile_of = [v.alloc_register(f"tile_of{k}") for k in range(G)]

            def add_items(L):
                acc, W = ((acc1, D), (acc2, H))[L]

                def add_group(n, s_, more):
                    i = n * R + s_
                    v.load(tile_of, tables[0:1, ds(i, G)])
                    for k in range(G):
                        if k or not more:
                            v.wait_ge(item_added[L], i + k)
                        else:
                            v.wait_ge(item_ready[L], n * (R // G) + (s_ + U) // G)
                        v.wait_ge(item_summed[L], i + (k + 1))
                        t = v.snap(tile_of[k], min_val=0, max_val=TILES - 1)
                        v.tensor_tensor(tile(acc, t), tile(acc, t), sum_bank[L][(s_ + k) % len(sum_bank[L])][:, 0:W], ALU.add).then_inc(item_added[L], 1)
                        if more:
                            if k == G - 1:
                                sources(L, i + R, s_)
                            target(L, i + (U + k), s_ % U + k)

                with v.Fori(0, TURNS) as n:
                    for s_ in range(0, R, G):
                        add_group(n, s_, True)
                for s_ in range(0, U, G):
                    add_group(TURNS, s_, False)

            v.wait_ge(cols_made, 2)
            first_items(0)
            v.tensor_scalar(scale1[:, :], scale1[:, :], 1.0, None, ALU.add).then_inc(scaled, 1)
            v.tensor_scalar(scale2[:, :], scale2[:, :], 1.0, None, ALU.add).then_inc(scaled, 1)
            v.wait_ge(scaled, 2)
            v.wait_ge(xn_put, 16 * GROUPS)
            then(v.tensor_scalar(acc1, acc1, scale1[:, :], None, ALU.mult))
            v.wait_ge(tables_in, 16)
            add_items(0)
            v.wait_ge(idx_ready[0], (ITEMS + U) // G)
            v.wait_ge(item_ready[0], ITEMS // G)
            for s_ in range(R):
                v.wait_ge(gathered[0][s_], 16 * (TURNS + 1 - s_ // U))
            first_items(1)
            v.tensor_tensor(xs[:, :, :], xs[:, :, :],
                            b2b_all[:, :].rearrange("p (t d) -> p t d", t=1).to_broadcast([P, TILES, D]),
                            ALU.add).then_inc(residual_ready, 1)
            v.wait_ge(g_scaled, TILES)
            add_items(1)

            statistics(stats_made, xs, TILES, ready=down_free[1])
            rstd_of(x2_root, x2_var)
            def norm_group(g):
                if g == 0:
                    v.wait_ge(staged[1], TILES)
                for t in range(g * GT, g * GT + GT):
                    ins = v.tensor_scalar(rows[:, t, 0:D], xs[:, t, :], mv[:, t, 0:1], ln[:, 4, t:t + 1],
                                          ALU.subtract, ALU.mult)
                ins.then_inc(xn2_made, 1)

            def pick_group(g):
                ts = slice(g * GT, g * GT + GT)
                v.wait_ge(gate_sum, g + 1)
                ins = v.tensor_tensor(gates[:, ts, :], bank[6][:, 0:GT * E].rearrange("p (t e) -> p t e", e=E),
                                      bg_all[:, :].rearrange("p (t e) -> p t e", t=1).to_broadcast([P, GT, E]), ALU.add)
                ins.then_inc(gate_out, 1)
                v.wait_ge(gate_out, g + 1)
                for t in range(g * GT, g * GT + GT):
                    ins = v.max(top[:, t, :], gates[:, t, :])
                then(ins)
                for t in range(g * GT, g * GT + GT):
                    ins = v.max_index(top_i[:, t, :], top[:, t, :], gates[:, t, :])
                then(ins)
                then(v.tensor_copy(top[:, ts, :], top_i[:, ts, :]))
                v.tensor_copy(rows[:, ts, D + 1:D + 2], top[:, ts, 0:1])
                for k, pick in enumerate((first, second)):
                    ins = v.tensor_tensor(pick[:, ts, :], expert_id[:, :, :], top[:, ts, k:k + 1].to_broadcast([P, GT, E]),
                                          ALU.is_equal)
                then(ins)
                if g == GROUPS - 1:
                    then(v.tensor_tensor(either[:, ts, :], first[:, ts, :], second[:, ts, :], ALU.add))
                    v.tensor_scalar(either[:, FULL, :], either[:, FULL, :], real[:, :], None, ALU.mult).then_inc(picked, 1)
                else:
                    v.tensor_tensor(either[:, ts, :], first[:, ts, :], second[:, ts, :], ALU.add).then_inc(picked, 1)

            def place_group(g):
                ts = slice(g * GT, g * GT + GT)
                v.wait_ge(placed, 2 * g + 2)
                then(v.tensor_copy(total[:, ts, :], bank[1][:, 0:GT * E].rearrange("p (t e) -> p t e", e=E)))
                for e in range(E):
                    ins = v.tensor_tensor_scan(upto[:, g * GT + 1:g * GT + GT + 1, e], total[:, ts, e], total[:, ts, e],
                                               upto[:, g * GT, e:e + 1], ALU.add, ALU.bypass)
                then(ins)
                then(v.tensor_tensor(at[:, ts, :], bank[0][:, 0:GT * E].rearrange("p (t e) -> p t e", e=E), upto[:, ts, :],
                                     ALU.add))
                for pick in (first, second):
                    ins = v.tensor_tensor(pick[:, ts, :], pick[:, ts, :], at[:, ts, :], ALU.mult)
                then(ins)
                for k, pick in enumerate((first, second)):
                    ins = v.tensor_reduce(slot[:, k, ts], pick[:, ts, :], AX_X, ALU.add)
                then(ins)
                v.tensor_copy(slot_i[:, :, ts], slot[:, :, ts]).then_inc(slots_made, 1)

            v.tensor_scalar(real[:, :], row_of[:, :], float(TAIL), None, ALU.is_lt)
            then(v.tensor_copy(upto[:, 0, :], region[:, :]))
            norm_group(0)
            for g in range(GROUPS):
                if g + 1 < GROUPS:
                    norm_group(g + 1)
                pick_group(g)
                place_group(g)

            v.tensor_copy(ends_i[:, :], upto[:, TILES, :]).then_inc(ends_made, 1)
            n_e, blocks_e, end_e, row_e, gap_e = (per_expert[:, k, :] for k in range(5))
            v.memset(turns[:, BTURNS_MIN % 2:BTURNS_MIN % 2 + 1], float(BTURNS_MIN - 2))
            then(v.tensor_tensor(n_e, upto[:, TILES, :], region[:, :], ALU.subtract))
            then(v.tensor_scalar(blocks_i[:, :], n_e, float(P - 1), None, ALU.add))
            then(v.tensor_scalar(blocks_i[:, :], blocks_i[:, :], 7, None, ALU.arith_shift_right))
            then(v.tensor_copy(blocks_e, blocks_i[:, :]))
            then(v.tensor_tensor_scan(end_e, blocks_e, blocks_e, 0.0, ALU.add, ALU.bypass))
            v.tensor_scalar(row_e, end_e, float(P), None, ALU.mult)
            for n in range(BTURNS_MIN, BTURNS):
                then(v.scalar_tensor_tensor(out=turns[:, (n + 1) % 2:(n + 1) % 2 + 1], in0=end_e[:, E - 1:E], scalar=float(n * UB),
                                            in1=turns[:, n % 2:n % 2 + 1], op0=ALU.is_gt, op1=ALU.add))
            then(v.tensor_scalar(gap_e, blocks_e, -1.0, float(RB), ALU.mult, ALU.add))
            then(v.memset(gap_e[:, E - 1:E], float(E * RB)))
            for e in range(E):
                v.tensor_scalar(block_cmp[:, 0, :, e], block_row[:, :], row_e[:, e:e + 1], None, ALU.is_ge)
                ins = v.tensor_scalar(block_cmp[:, 1, :, e], block_row[:, :], row_e[:, e:e + 1], gap_e[:, e:e + 1],
                                      ALU.is_ge, ALU.mult)
            then(ins)
            v.tensor_reduce(block_expert[:, :], block_cmp[:, 0, :, 0:E - 1], AX_X, ALU.add)
            then(v.tensor_reduce(block_pos[:, 0, :], block_cmp[:, 1, :, :], AX_X, ALU.add))
            v.tensor_copy(block_expert_i[:, :], block_expert[:, :])
            v.tensor_copy(turns_i[:, :], turns[:, BTURNS % 2:BTURNS % 2 + 1])
            then(v.scalar_tensor_tensor(out=block_pos[:, 1, :], in0=block_row[:, :], scalar=1.0 / P, in1=block_pos[:, 0, :],
                                        op0=ALU.mult, op1=ALU.add))
            v.tensor_scalar(block_pos_i[:, :], block_pos[:, 1, :], float(E * RB), None, ALU.min).then_inc(blocks_made, 1)
            v.wait_ge(blocks_made, 1)

            def prepare(m, c):
                i, u = m * UB + c, c % UB
                v.wait_ge(block_in[u], m * 16 + (c // UB + 1) * 16)
                node, expert = xb[:, u, D:D + 1], xb[:, u, D + 1:D + 2]
                v.tensor_scalar(dest[:, 0, ds(i, 1)], expert, block_expert[:, ds(i, 1)], float(NP), ALU.not_equal, ALU.mult)
                v.scalar_tensor_tensor(out=dest[:, 1, ds(i, 1)], in0=expert, scalar=0.0, in1=block_row[:, ds(i, 1)],
                                       op0=ALU.is_lt, op1=ALU.mult)
                v.tensor_copy(dest[:, 2, ds(i, 1)], node).then_inc(dest_made, 1)
                e = v.value_load(block_expert_i[0:1, ds(i, 1)], min_val=0, max_val=E - 1)
                if c >= UB:
                    v.wait_ge(bh, m * UB + (c + 1 - UB))
                v.tensor_copy(w_now[u], we1[:, ds(e, 1), :, :].rearrange("p e k n -> p (e k) n")).then_inc(w_copied, 1)

            def take_y(m, c):
                i, u = m * UB + c, c % UB
                e = v.value_load(block_expert_i[0:1, ds(i, 1)], min_val=0, max_val=E - 1)
                v.wait_ge(dest_made, m * UB + (c + 1))
                if c >= UB:
                    v.wait_ge(block_put[u], m * 16 + (c // UB) * 16)
                v.scalar_tensor_tensor(out=dest_i[:, u:u + 1], in0=dest[:, 0, ds(i, 1)], scalar=dest[:, 1, ds(i, 1)],
                                       in1=dest[:, 2, ds(i, 1)], op0=ALU.add, op1=ALU.add)
                v.wait_ge(by, m * UB + (c + 1))
                v.tensor_tensor(yb[:, u, :], bank[5 + u][:, 0:D], tile(b2_all, e), ALU.add).then_inc(by_out, 1)

            middle = middle_turns(v)
            v.wait_ge(expert1_in, 16)
            v.wait_ge(bias2_in, 16)
            for c in range(UB):
                prepare(0, c)
            for c in range(UB):
                prepare(0, c + UB)
                take_y(0, c)
            with v.Fori(0, middle) as m:
                for c in range(UB, 2 * UB):
                    prepare(m, c + UB)
                    take_y(m, c)
            for c in range(UB, 2 * UB):
                take_y(middle, c)

            for g, (t0, t1, n) in enumerate(parts_out):
                v.wait_ge(ys_in[g], 32)
                v.tensor_tensor(xs[0:n, t0:t1, :], xs[0:n, t0:t1, :], ys[0:n, 0, t0:t1, :], ALU.add).then_inc(first_added, 1)
                v.wait_ge(first_added, g + 1)
                v.tensor_tensor(xs[0:n, t0:t1, :], xs[0:n, t0:t1, :], ys[0:n, 1, t0:t1, :], ALU.add).then_inc(summed, 1)


_INS = ['x', 'src', 'dst', 'L0_gnn_W1a', 'L0_gnn_b1a', 'L0_gnn_W1b', 'L0_gnn_b1b', 'L0_gnn_W2a', 'L0_gnn_b2a',
        'L0_gnn_W2b', 'L0_gnn_b2b', 'L0_gnn_eps1', 'L0_gnn_eps2', 'L0_ffn_Wg', 'L0_ffn_bg', 'L0_ffn_W1', 'L0_ffn_b1',
        'L0_ffn_W2', 'L0_ffn_b2']


def kernel(**inputs):
    import numpy as _np
    import concourse.bacc as _bacc
    from concourse import mybir as _mybir
    from concourse.bass_utils import run_bass_kernel_spmd as _run

    nc = _bacc.Bacc("TRN2", target_bir_lowering=False, num_devices=1)
    arrays, args = {}, []
    for name in _INS:
        a = _np.ascontiguousarray(inputs[name]).reshape(_np.shape(inputs[name]) or (1,))
        arrays[f"in_{name}_dram"] = a
        args.append(nc.dram_tensor(f"in_{name}_dram", a.shape, _mybir.dt.from_np(a.dtype), kind="ExternalInput").ap())
    shape = tuple(inputs["x"].shape)
    args.append(nc.dram_tensor("out_0_dram", shape, _mybir.dt.float32, kind="ExternalOutput").ap())
    gnn_moe_kernel(nc, *args)
    r = _run(nc, [arrays], core_ids=[0])
    return r.results[0]["out_0_dram"]
```
